# Optimizing a Trainium2 kernel written in Bass

```python
import numpy as np
import jax
import jax.numpy as jnp

def _softmax(x, axis=-1):
    return jax.nn.softmax(x, axis=axis)

def _gelu(x):
    return jax.nn.gelu(x, approximate=True)

def _silu(x):
    return jax.nn.silu(x)

def _sigmoid(x):
    return jax.nn.sigmoid(x)

def _layernorm(x, axis=-1, eps=1e-05):
    m = jnp.mean(x, axis=axis, keepdims=True)
    v = jnp.var(x, axis=axis, keepdims=True)
    return (x - m) / jnp.sqrt(v + eps)

def _scatter_add(tgt, idx, src, axis=0):
    return tgt.at[idx].add(src)

def _segment_sum(src, seg, n):
    return jax.ops.segment_sum(src, seg, n)
kernel_name = 'mk_early_fusion_d1_tok_img768_r4_c3cc66'

def setup_inputs(seed: int=0):
    np.random.seed(seed)
    _w = jnp.asarray

    def _rec_inputs():
        import jax
        import jax.numpy as jnp
        _rk = jax.random.key(seed)
        x = 1.64766e-05 + 1.00005 * jax.random.normal(jax.random.fold_in(_rk, 1), (8, 3, 512, 192), jnp.float32)
        txt = -0.000331106 + 0.408041 * jax.random.normal(jax.random.fold_in(_rk, 2), (8, 32, 192), jnp.float32)
        return (x, txt)
    x, txt = _rec_inputs()

    def _L0_tok_setup():
        import jax, jax.numpy as jnp
        import numpy as np
        NUM_BANDS = 6
        D_MODEL = 192
        B, N = (2, 512)
        IN_FEATURES = 3 * NUM_BANDS * 2 * D_MODEL
        key = jax.random.key(seed)
        k_xyz, k_w = jax.random.split(key)
        xyz = jax.random.normal(k_xyz, (B, 3, N, D_MODEL), dtype=jnp.float32)
        freq_bands = 2.0 ** jnp.linspace(0.0, NUM_BANDS - 1, NUM_BANDS).astype(jnp.float32)
        bound = 1.0 / np.sqrt(IN_FEATURES)
        W = jax.random.uniform(k_w, (D_MODEL, IN_FEATURES), dtype=jnp.float32, minval=-bound, maxval=bound)
        return {'xyz': xyz, 'freq_bands': freq_bands, 'W': W}
    _L0_tok_all = _L0_tok_setup()
    _L0_tok_in = {k: v for k, v in _L0_tok_all.items() if k in ('freq_bands', 'W')}
    del _L0_tok_all

    def _L0_attn_setup():
        import jax, jax.numpy as jnp
        import numpy as np
        INIT_STD = 0.05
        key = jax.random.key(seed)
        k1, k2, k3 = jax.random.split(key, 3)
        b, p, d = (2, 512, 192)
        h, n = (12, 64)
        x = jax.random.normal(k1, (b, p, d), dtype=jnp.float32)
        w_qkv = INIT_STD * jax.random.normal(k2, (h, 3, d, n), dtype=jnp.float32)
        w_o = INIT_STD * jax.random.normal(k3, (h * n, d), dtype=jnp.float32)
        return {'x': x, 'w_qkv': w_qkv, 'w_o': w_o}
    _L0_attn_all = _L0_attn_setup()
    _L0_attn_in = {k: v for k, v in _L0_attn_all.items() if k in ('w_qkv', 'w_o')}
    del _L0_attn_all

    def _L0_ffn_setup():
        import jax, jax.numpy as jnp
        import numpy as np
        key = jax.random.key(seed)
        ks = jax.random.split(key, 6)
        B, N, D, E, S, H = (4, 1024, 192, 4, 256, 768)
        sc = lambda d: 1.0 / np.sqrt(d)
        return {'x': jax.random.normal(ks[0], (B, N, D), dtype=jnp.float32), 'phi': jax.random.normal(ks[1], (E, S, D), dtype=jnp.float32) * sc(D), 'w1': jax.random.normal(ks[2], (E, D, H), dtype=jnp.float32) * sc(D), 'b1': jnp.zeros((E, H), dtype=jnp.float32), 'w2': jax.random.normal(ks[3], (E, H, D), dtype=jnp.float32) * sc(H), 'b2': jnp.zeros((E, D), dtype=jnp.float32)}
    _L0_ffn_all = _L0_ffn_setup()
    _L0_ffn_in = {k: v for k, v in _L0_ffn_all.items() if k in ('phi', 'w1', 'b1', 'w2', 'b2')}
    del _L0_ffn_all
    return {'x': x, 'txt': txt, 'L0_tok_freq_bands': _L0_tok_in['freq_bands'], 'L0_tok_W': _L0_tok_in['W'], 'L0_attn_w_qkv': _L0_attn_in['w_qkv'], 'L0_attn_w_o': _L0_attn_in['w_o'], 'L0_ffn_phi': _L0_ffn_in['phi'], 'L0_ffn_w1': _L0_ffn_in['w1'], 'L0_ffn_b1': _L0_ffn_in['b1'], 'L0_ffn_w2': _L0_ffn_in['w2'], 'L0_ffn_b2': _L0_ffn_in['b2']}

def reference(x, txt, L0_tok_freq_bands, L0_tok_W, L0_attn_w_qkv, L0_attn_w_o, L0_ffn_phi, L0_ffn_w1, L0_ffn_b1, L0_ffn_w2, L0_ffn_b2):
    import jax
    import jax.numpy as jnp

    def _L0_tok_ref(xyz, freq_bands, W):
        import jax, jax.numpy as jnp
        import numpy as np
        NUM_BANDS = 6
        D_MODEL = 192
        B, N = (2, 512)
        IN_FEATURES = 3 * NUM_BANDS * 2 * D_MODEL
        b, c, n, d = xyz.shape
        xb = 2.0 * jnp.pi * xyz[..., None] * freq_bands
        feat = jnp.concatenate([jnp.sin(xb), jnp.cos(xb)], axis=-1)
        feat = feat.reshape(b, n, -1)
        return jnp.einsum('bnf,of->bno', feat, W)

    def _L0_attn_ref(x, w_qkv, w_o):
        import jax, jax.numpy as jnp
        import numpy as np
        INIT_STD = 0.05
        head_dim = w_qkv.shape[-1]
        qkv = jnp.einsum('bpv,havn->bhapn', x, w_qkv)
        q, k, v = (qkv[:, :, 0], qkv[:, :, 1], qkv[:, :, 2])
        scale = jnp.sqrt(jnp.asarray(head_dim, dtype=x.dtype))
        scores = jnp.einsum('bhqn,bhkn->bhqk', q, k) / scale
        attn = jax.nn.softmax(scores, axis=-1)
        out = jnp.einsum('bhqk,bhkn->bhqn', attn, v)
        b, h, p, n = out.shape
        out = out.transpose(0, 2, 1, 3).reshape(b, p, h * n)
        return jnp.einsum('bpi,ij->bpj', out, w_o)

    def _L0_ffn_ref(x, phi, w1, b1, w2, b2):
        import jax, jax.numpy as jnp
        import numpy as np
        logits = jnp.einsum('bnd,esd->bnes', x, phi)
        B, N, E, S = logits.shape
        dispatch = jax.nn.softmax(logits, axis=1)
        combine = jax.nn.softmax(logits.reshape(B, N, E * S), axis=-1).reshape(B, N, E, S)
        slots = jnp.einsum('bnd,bnes->besd', x, dispatch)
        h = jax.nn.gelu(jnp.einsum('besd,edh->besh', slots, w1) + b1[None, :, None, :])
        y = jnp.einsum('besh,ehd->besd', h, w2) + b2[None, :, None, :]
        out = jnp.einsum('besd,bnes->bnd', y, combine)
        return out
    h = _L0_tok_ref(x, L0_tok_freq_bands, L0_tok_W)
    h = jnp.concatenate([h, txt], axis=1)
    h = h + _L0_attn_ref(_layernorm(h, axis=-1), L0_attn_w_qkv, L0_attn_w_o)
    h = h + _L0_ffn_ref(_layernorm(h, axis=-1), L0_ffn_phi, L0_ffn_w1, L0_ffn_b1, L0_ffn_w2, L0_ffn_b2)
    return h

_drawn_inputs = setup_inputs


def setup_inputs(seed=0):
    import zlib

    import numpy as np

    out = dict(_drawn_inputs(seed))
    spreads = {'L0_ffn_b1': (0.0, 0.1), 'L0_ffn_b2': (0.0, 0.1)}
    factors = {'L0_ffn_phi': 4.714}
    for name, (base, spread) in spreads.items():
        noise = np.random.default_rng([zlib.crc32(name.encode()), seed]).standard_normal(out[name].shape)
        drawn = base * np.exp(spread * noise) if base else spread * noise
        out[name] = jnp.asarray(drawn.astype(out[name].dtype))
    for name, factor in factors.items():
        out[name] = (out[name] * factor).astype(out[name].dtype)
    return out
```

```python
from contextlib import ExitStack

import concourse.bass as bass
from concourse import mybir

F32 = mybir.dt.float32
F32R = mybir.dt.float32r
ACT = mybir.ActivationFunctionType
ALU = mybir.AluOpType
AXX = mybir.AxisListType.X
AXXY = mybir.AxisListType.XY

P = 128
NB, NX, NT, D = 8, 512, 32, 192
N = NX + NT
TQ = [128, 128, 128, 128, 32]
NTILE = len(TQ)
HALF = N // 2
D1 = D - P
BANDS = 6
CH = 5
NKU = (CH - 1) * 2 * BANDS + BANDS
EPS = 1e-5
MAGIC = 12582912.0
TWO_PI = 6.2831845
HALF_PI = 1.5707963

NH, HD = 12, 64
NP = NH // 2
NE, NS, FH = 4, 256, 768
ES = NE * NS
NM = ES // P
FM = FH // P


class Tally:

    def __init__(self, sem, per):
        self.sem, self.per = sem, per

    def start(self, eng):
        eng.sem_inc(self.sem, self.per)

    def wait(self, eng, it, k):
        eng.wait_ge(self.sem, it * self.per + (self.per + k))


def tok_phase(nc, sem, h, aps):
    x_d, w_d, f_d, txt_d = aps
    NU = CH * 3
    SLOTS = 3
    made = [0]
    for u in range(NU):
        made.append(made[-1] + (2 if u // 3 < CH - 1 else 1))
    with ExitStack() as ctx:
        def sb(name, shape, dt=F32):
            return ctx.enter_context(nc.sbuf_tensor(name, shape, dt))
        w = sb("tok_w", [P, NKU, D])
        freq = sb("tok_freq", [P, BANDS])
        x = sb("tok_x", [P, CH, NX])
        shifted = sb("tok_shifted", [P, 2, NX])
        whole = sb("tok_whole", [P, 2, NX])
        turn = sb("tok_turn", [P, SLOTS, 2, NX])
        absturn = sb("tok_absturn", [P, SLOTS, 2, NX])
        feat = sb("tok_feat", [P, SLOTS, 2, 2, NX])
        sc = sb("tok_sc", [P, 3])
        acc = [ctx.enter_context(nc.psum_tensor(f"tok_acc{t}", [P, 512], F32)) for t in range(4)]

        w_in = sem("tok_w_in")
        f_in = sem("tok_f_in")
        txt_in = sem("tok_txt_in")
        const_ok = sem("tok_const_ok")
        x_in = [Tally(sem(f"tok_x_in{c}"), 16) for c in range(CH)]
        x_used = Tally(sem("tok_x_used"), CH)
        shifted_ok = Tally(sem("tok_shifted_ok"), 2 * NU)
        whole_ok = Tally(sem("tok_whole_ok"), NU)
        turn_ok = Tally(sem("tok_turn_ok"), 2 * NU)
        abs_ok = Tally(sem("tok_abs_ok"), NU)
        feat_ok = Tally(sem("tok_feat_ok"), made[-1])
        feat_used = Tally(sem("tok_feat_used"), NU)
        acc_ok = Tally(sem("tok_acc_ok"), 3)
        acc_out = Tally(sem("tok_acc_out"), 4)
        block = ctx.enter_context(nc.Block())

        @block.sync
        def _(sp):
            for c in range(CH):
                x_in[c].start(sp)
            sp.dma_start(freq[:, :], f_d).then_inc(f_in, 16)
            for c in range(CH):
                sp.dma_start(x[:, c, :], x_d[0, c]).then_inc(x_in[c].sem, 16)
            sp.dma_start(w[:, :, :].rearrange("p k n -> p (k n)"), w_d).then_inc(w_in, 16)
            sp.dma_start(h[0:NT, NTILE - 1:NB * NTILE:NTILE, :],
                         txt_d.rearrange("b n d -> n b d")).then_inc(txt_in, 16)
            with sp.Fori(0, NB - 1) as b:
                for c in range(CH):
                    src = x_d[bass.ds(b + 1, 1), c].rearrange("o p n -> (o p) n")
                    x_used.wait(sp, b, c + 1)
                    sp.dma_start(x[:, c, :], src).then_inc(x_in[c].sem, 16)
            sp.wait_ge(w_in, 16)
            sp.wait_ge(txt_in, 16)

        @block.vector
        def _(dve):
            for s in (x_used, shifted_ok, whole_ok, turn_ok, abs_ok):
                s.start(dve)
            dve.memset(sc[0:D1, 0:1], TWO_PI)
            dve.memset(sc[D1:P, 0:1], -TWO_PI)
            dve.memset(sc[0:D1, 1:2], 0.0)
            dve.memset(sc[D1:P, 1:2], HALF_PI)
            dve.memset(sc[:, 2:3], HALF_PI).then_inc(const_ok, 1)
            dve.wait_ge(f_in, 16)
            with dve.Fori(0, NB) as b:
                for u in range(NU):
                    c, jp, s = u // 3, u % 3, u % SLOTS
                    if jp == 0:
                        x_in[c].wait(dve, b, 16)
                    turn_ok.wait(dve, b, 2 * u)
                    for jj in range(2):
                        j = 2 * jp + jj
                        dve.tensor_scalar(shifted[:, jj, :], x[:, c, :], freq[:, j:j + 1], MAGIC,
                                          ALU.mult, ALU.add).then_inc(shifted_ok.sem, 1)
                    shifted_ok.wait(dve, b, 2 * u + 2)
                    dve.tensor_scalar(whole[:, :, :], shifted[:, :, :], MAGIC, None,
                                      ALU.subtract).then_inc(whole_ok.sem, 1)
                    whole_ok.wait(dve, b, u + 1)
                    prev = u - SLOTS
                    feat_ok.wait(dve, b, made[prev + 1] if prev >= 0 else made[prev + NU + 1] - made[-1])
                    for jj in range(2):
                        j = 2 * jp + jj
                        dve.scalar_tensor_tensor(turn[:, s, jj, :], x[:, c, :], freq[:, j:j + 1],
                                                 whole[:, jj, :], ALU.mult,
                                                 ALU.subtract).then_inc(turn_ok.sem, 1)
                    turn_ok.wait(dve, b, 2 * u + 2)
                    if c < CH - 1:
                        dve.scalar_tensor_tensor(absturn[:, s, :, :], turn[:, s, :, :], -1.0, turn[:, s, :, :],
                                                 ALU.mult, ALU.max).then_inc(abs_ok.sem, 1)
                    else:
                        dve.scalar_tensor_tensor(turn[D1:P, s, :, :], turn[D1:P, s, :, :], -1.0,
                                                 turn[D1:P, s, :, :], ALU.mult,
                                                 ALU.max).then_inc(abs_ok.sem, 1)
                    if jp == 2:
                        dve.sem_inc(x_used.sem, 1)

        @block.scalar
        def _(act):
            feat_ok.start(act)
            acc_out.start(act)
            act.wait_ge(const_ok, 1)
            with act.Fori(0, NB) as b:
                for u in range(NU):
                    c, s = u // 3, u % SLOTS
                    feat_used.wait(act, b, u - SLOTS + 1)
                    if c < CH - 1:
                        turn_ok.wait(act, b, 2 * u + 2)
                        act.activation(feat[:, s, 0, :, :], turn[:, s, :, :], ACT.Sin,
                                       scale=TWO_PI).then_inc(feat_ok.sem, 1)
                        abs_ok.wait(act, b, u + 1)
                        act.activation(feat[:, s, 1, :, :], absturn[:, s, :, :], ACT.Sin, bias=sc[:, 2:3],
                                       scale=-TWO_PI).then_inc(feat_ok.sem, 1)
                    else:
                        abs_ok.wait(act, b, u + 1)
                        act.activation(feat[:, s, 0, :, :], turn[:, s, :, :], ACT.Sin, bias=sc[:, 1:2],
                                       scale=sc[:, 0:1]).then_inc(feat_ok.sem, 1)
                for t in range(4):
                    if t < 3:
                        acc_ok.wait(act, b, t + 1)
                    else:
                        feat_used.wait(act, b, NU)
                    act.activation(h[:, bass.ds(b * NTILE + t, 1), :].rearrange("p o d -> p (o d)"),
                                   acc[t][:, 0:D], ACT.Copy).then_inc(acc_out.sem, 1)

        @block.tensor
        def _(pe):
            feat_used.start(pe)
            acc_ok.start(pe)
            pe.wait_ge(w_in, 16)
            with pe.Fori(0, NB) as b:
                k = 0
                for u in range(NU):
                    c, s = u // 3, u % SLOTS
                    for kind in range(2 if c < CH - 1 else 1):
                        feat_ok.wait(pe, b, made[u] + kind + 1)
                        for jj in range(2):
                            for t in range(4):
                                if k == 0:
                                    acc_out.wait(pe, b, t - 3)
                                last = pe.matmul(acc[t][:, 0:D], feat[:, s, kind, jj, t * P:(t + 1) * P],
                                                 w[:, k, :], start=(k == 0), stop=(k == NKU - 1))
                                if k == NKU - 1 and t < 3:
                                    last.then_inc(acc_ok.sem, 1)
                            k += 1
                    last.then_inc(feat_used.sem, 1)



def layernorm(dve, pool, h, b, hn, stats, mv, rstd, ln):
    if dve is not None:
        for t, tq in enumerate(TQ):
            row = h[0:tq, bass.ds(b * NTILE + t, 1), :].rearrange("p o d -> p (o d)")
            dve.bn_stats(stats[0:tq, t, :], row).then_inc(ln.stats.sem, 1)
        for t, tq in enumerate(TQ):
            ln.stats.wait(dve, b, t + 1)
            take_wait(dve, ln.taken)
            dve.bn_aggr(mv[0:tq, t, :], stats[0:tq, t, :]).then_inc(ln.mv.sem, 1)
        ln.rstd.wait(dve, b, 2)
        for t, tq in enumerate(TQ):
            for c0, c1, o in ((0, D, 0), (P, D, D)):
                if o + c1 - c0 > hn.shape[2]:
                    continue
                row = h[0:tq, bass.ds(b * NTILE + t, 1), c0:c1].rearrange("p o d -> p (o d)")
                dve.tensor_scalar(hn[0:tq, t, o:o + c1 - c0], row, mv[0:tq, t, 0:1], rstd[0:tq, 1, t:t + 1],
                                  ALU.subtract, ALU.mult).then_inc(ln.hn.sem, 1)
    if pool is not None:
        ln.mv.wait(pool, b, NTILE)
        take_wait(pool, ln.taken)
        pool.tensor_scalar(rstd[:, 0, :], mv[:, :, 1], EPS, None, ALU.add).then_inc(ln.rstd.sem, 1)
        ln.rstd.wait(pool, b, 1)
        pool.tensor_tensor(rstd[:, 1, :], rstd[:, 0, :], rstd[:, 2, :], ALU.pow).then_inc(ln.rstd.sem, 1)


def take_wait(eng, taken):
    eng.sem_inc(taken, 1)


class LnSems:

    def __init__(self, sem, name, hn_ops):
        self.stats = Tally(sem(name + "_stats"), NTILE)
        self.mv = Tally(sem(name + "_mv"), NTILE)
        self.rstd = Tally(sem(name + "_rstd"), 2)
        self.hn = Tally(sem(name + "_hn"), hn_ops)
        self.taken = sem(name + "_taken")


def attn_order():
    steps = [("TR", 0), ("TR", 1)] + [("V", t) for t in range(NTILE)] + [("QK", 0, 0), ("QK", 0, 1)]
    for n in range(NH + 2):
        for i in range(NTILE):
            if 0 <= n - 1 < NH:
                steps.append(("T", n - 1, i))
            if n < NH:
                steps.append(("S", n, i))
            if 0 <= n - 1 < NH and i >= 2:
                steps.append(("PV", n - 1, i - 2))
            if i == 1 and 0 <= n - 2:
                steps.append(("Y", n - 2))
            if i in (2, 3) and n % 2 == 0 and n // 2 + 1 < NP:
                steps.append(("QK", n // 2 + 1, i - 2))
        if 0 <= n - 1 < NH:
            steps += [("T", n - 1, 5), ("PV", n - 1, 3), ("PV", n - 1, 4)]
    return steps


def attn_phase(nc, sem, h, aps):
    w0_d, w1_d, wo_d = aps
    W3 = 3 * NH * HD
    steps = attn_order()
    slot_of = {s: i for i, s in enumerate(x for x in steps if x[0] in ("TR", "V", "QK", "S", "Y"))}
    bank_of = {s: i for i, s in enumerate(x for x in steps if x[0] in ("T", "Y"))}
    slot_users = list(slot_of)
    dve_steps = list(steps)
    for j in range(1, len(steps)):
        if steps[j - 1][0] == "T" and steps[j][0] == "S":
            dve_steps[j - 1:j + 1] = [steps[j], steps[j - 1]]
    NSLOT, NBANK = len(slot_of), len(bank_of)
    with ExitStack() as ctx:
        def sb(name, shape, dt=F32):
            return ctx.enter_context(nc.sbuf_tensor(name, shape, dt))

        def ps(name, shape):
            return ctx.enter_context(nc.psum_tensor(name, shape, F32))
        ident = sb("at_ident", [P, P])
        hn = sb("at_hn", [P, NTILE, 2 * P])
        stats = sb("at_stats", [P, NTILE, 6])
        mv = sb("at_mv", [P, NTILE, 2])
        rstd = sb("at_rstd", [P, 3, NTILE])
        x0h, x0l, x1s = (sb(n, [P, N], F32R) for n in ("at_x0h", "at_x0l", "at_x1s"))
        w0h, w0l, w1h = (sb(n, [P, W3], F32R) for n in ("at_w0h", "at_w0l", "at_w1h"))
        w1l = sb("at_w1l", [D1, W3], F32R)
        woh, wol = (sb(n, [P, NH, D], F32R) for n in ("at_woh", "at_wol"))
        qk_h = sb("at_qk_h", [P, 2, N], F32R)
        q_l = sb("at_q_l", [P, N], F32R)
        k_l = sb("at_k_l", [P, 2, N], F32R)
        q_s = sb("at_q_s", [P, 2, 2, N], F32R)
        k_s = sb("at_k_s", [P, 2, 2, N], F32R)
        v_s = sb("at_v_s", [P, NTILE, NH, 2 * HD], F32R)
        prob = sb("at_prob", [P, 2, NTILE, N])
        pt_h, pt_l = (sb(n, [P, NTILE, N], F32R) for n in ("at_pt_h", "at_pt_l"))
        o_h, o_l = (sb(n, [P, N], F32R) for n in ("at_o_h", "at_o_l"))
        negmax, rowsum, rinv = (sb(n, [P, NH, NTILE]) for n in ("at_negmax", "at_rowsum", "at_rinv"))
        slots = [ps(f"at_slot{i}", [P, 2, 512]) for i in range(2)]
        banks = [ps(f"at_bank{i}", [P, 512]) for i in range(2)]
        o_ps = ps("at_o", [P, 2, 512])
        stage = prob[:, :, :, :].rearrange("p a t n -> p (a t n)")

        w_in = [sem(f"at_w_in{i}") for i in range(3)]
        ident_ok = sem("at_ident_ok")
        w_hi, w_lo, w_sent = sem("at_w_hi"), sem("at_w_lo"), sem("at_const")
        ln = LnSems(sem, "at_ln", 2 * NTILE)
        slot_full = Tally(sem("at_slot_full"), NSLOT)
        bank_full = Tally(sem("at_bank_full"), NBANK)
        o_full = Tally(sem("at_o_full"), NH)
        tr_h, tr_l = Tally(sem("at_tr_h"), 2), Tally(sem("at_tr_l"), 2)
        v_h, v_l = Tally(sem("at_v_h"), NTILE), Tally(sem("at_v_l"), NTILE)
        proj_h, proj_l = Tally(sem("at_proj_h"), NH), Tally(sem("at_proj_l"), NH)
        stacked = [Tally(sem(f"at_stacked{i}"), NP // 2 * 128) for i in range(2)]
        max_ok = Tally(sem("at_max_ok"), NH * NTILE)
        exp_ok = Tally(sem("at_exp_ok"), NH * NTILE)
        ptr_h, ptr_l = Tally(sem("at_ptr_h"), NH * 6), Tally(sem("at_ptr_l"), NH * 6)
        out_h, out_l = Tally(sem("at_out_h"), NH), Tally(sem("at_out_l"), NH)
        rinv_ok = Tally(sem("at_rinv_ok"), NH)
        added = Tally(sem("at_added"), 2 * NH)
        taken = sem("at_taken")
        block = ctx.enter_context(nc.Block())

        def transposed(dst, k, i):
            bank = banks[k % 2]
            if i == 0:
                return [(dst[:, 0:4, NX:N], bank[:, 0:P].rearrange("p (t n) -> p t n", n=NT)),
                        (dst[0:NT, 4, NX:N], bank[0:NT, P:P + NT])]
            kw = TQ[i - 1]
            return [(dst[0:kw, i - 1, 0:NX], bank[0:kw, :])]

        def slot_view(k, tq, width):
            return slots[k % 2][0:tq, :, 0:width]

        def wait_slot_free(eng, b, k):
            for back in range(1, NSLOT + 1):
                if (k - back) % NSLOT % 2 == k % 2:
                    break
            unit = slot_users[(k - back) % NSLOT]
            kind = unit[0]
            tally, count = {
                "TR": lambda: (tr_l, unit[1] + 1),
                "V": lambda: (v_l, unit[1] + 1),
                "QK": lambda: (proj_l, 2 * unit[1] + unit[2] + 1),
                "S": lambda: (exp_ok, unit[1] * NTILE + unit[2] + 1),
                "Y": lambda: (added, 2 * unit[1] + 1),
            }[kind]()
            tally.wait(eng, b, count - (tally.per if k < back else 0))

        def wait_bank_free(eng, b, k):
            prev = (k - 2) % NBANK
            unit = list(bank_of)[prev]
            if unit[0] == "T":
                ptr_l.wait(eng, b, unit[1] * 6 + unit[2] + 1 - (ptr_l.per if k < 2 else 0))
            else:
                added.wait(eng, b, 2 * unit[1] + 2 - (added.per if k < 2 else 0))

        @block.sync
        def _(sp):
            for s in stacked:
                s.start(sp)
            sp.dma_start(stage[:, 0:W3], w0_d).then_inc(w_in[0], 16)
            sp.dma_start(stage[:, W3:2 * W3], w1_d).then_inc(w_in[1], 16)
            sp.wait_ge(w_lo, 2)
            sp.dma_start(stage[:, 0:NH * D], wo_d).then_inc(w_in[2], 16)
            with sp.Fori(0, NB) as b:
                for p in range(NP):
                    proj_l.wait(sp, b, 2 * p + 2)
                    s = stacked[p % 2].sem
                    a, z = slice(0, HD), slice(HD, P)
                    for dst, src in ((q_s[a, p % 2, 0], qk_h[a, 0]), (q_s[z, p % 2, 0], q_l[a]),
                                     (q_s[z, p % 2, 1], qk_h[z, 0]), (q_s[a, p % 2, 1], q_l[z]),
                                     (k_s[a, p % 2, 0], qk_h[a, 1]), (k_s[z, p % 2, 0], qk_h[a, 1]),
                                     (k_s[z, p % 2, 1], qk_h[z, 1]), (k_s[a, p % 2, 1], qk_h[z, 1])):
                        sp.dma_start(dst.bitcast(F32), src.bitcast(F32)).then_inc(s, 16)

        @block.gpsimd
        def _(pool):
            ln.rstd.start(pool)
            pool.memset(ident[:, :], 0.0).then_inc(ident_ok, 1)
            pool.memset(rstd[:, :, :], -0.5).then_inc(ident_ok, 1)
            pool.memset(mv[:, :, :], 1.0).then_inc(ident_ok, 1)
            pool.memset(rowsum[:, :, :], 1.0).then_inc(ident_ok, 1)
            pool.wait_ge(ident_ok, 4)
            pool.affine_select(out=ident[:, :], in_=ident[:, :], compare_op=ALU.not_equal, fill=1.0, base=0,
                               pattern=[[-1, P]], channel_multiplier=1).then_inc(ident_ok, 1)
            with pool.Fori(0, NB) as b:
                layernorm(None, pool, h, b, hn, stats, mv, rstd, ln)

        @block.scalar
        def _(act):
            for s in (tr_h, v_h, proj_h, exp_ok, ptr_h, out_h):
                s.start(act)
            act.wait_ge(w_in[0], 16)
            act.activation(w0h[:, :], stage[:, 0:W3], ACT.Copy).then_inc(w_hi, 1)
            act.wait_ge(w_in[1], 16)
            act.activation(w1h[:, :], stage[:, W3:2 * W3], ACT.Copy).then_inc(w_hi, 1)
            act.wait_ge(w_in[2], 16)
            act.activation(woh[:, :, :].rearrange("p h d -> p (h d)"), stage[:, 0:NH * D],
                           ACT.Copy).then_inc(w_hi, 1)
            act.wait_ge(ident_ok, 5)
            act.wait_ge(w_lo, 3)
            with act.Fori(0, NB) as b:
                for step in steps:
                    kind = step[0]
                    if kind == "TR":
                        slot_full.wait(act, b, slot_of[step] + 1)
                        src = slots[slot_of[step] % 2][:, :, :].rearrange("p a n -> p (a n)")[:, 0:N]
                        act.activation((x1s if step[1] else x0h)[:, :], src, ACT.Copy).then_inc(tr_h.sem, 1)
                    elif kind == "V":
                        t = step[1]
                        slot_full.wait(act, b, slot_of[step] + 1)
                        for a in range(2):
                            src = slots[slot_of[step] % 2][0:TQ[t], a, 0:6 * HD].rearrange("p (h n) -> p h n", n=HD)
                            last = act.activation(v_s[0:TQ[t], t, 6 * a:6 * a + 6, 0:HD], src, ACT.Copy)
                        last.then_inc(v_h.sem, 1)
                    elif kind == "QK":
                        p, m = step[1:]
                        slot_full.wait(act, b, slot_of[step] + 1)
                        stacked[(p - 1) % 2].wait(act, b, ((p - 1) // 2 + 1) * 128)
                        act.activation(qk_h[:, m, :].rearrange("p (a n) -> p a n", a=2), slot_view(slot_of[step], P, HALF),
                                       ACT.Copy, scale=(0.125 if m == 0 else 1.0)).then_inc(proj_h.sem, 1)
                    elif kind == "S":
                        n, i = step[1:]
                        tq = TQ[i]
                        max_ok.wait(act, b, n * NTILE + i + 1)
                        act.activation(prob[0:tq, n % 2, i, :].rearrange("p (a n) -> p a n", a=2),
                                       slot_view(slot_of[step], tq, HALF), ACT.Exp, bias=negmax[0:tq, n, i:i + 1],
                                       accum_out=rowsum[0:tq, n, i:i + 1]).then_inc(exp_ok.sem, 1)
                    elif kind == "T":
                        n, i = step[1:]
                        bank_full.wait(act, b, bank_of[step] + 1)
                        for dst, src in transposed(pt_h, bank_of[step], i):
                            last = act.activation(dst, src, ACT.Copy)
                        last.then_inc(ptr_h.sem, 1)
                    elif kind == "PV" and step[2] == NTILE - 1:
                        o_full.wait(act, b, step[1] + 1)
                        act.activation(o_h[:, :].rearrange("p (a n) -> p a n", a=2), o_ps[:, :, 0:HALF],
                                       ACT.Copy).then_inc(out_h.sem, 1)

        @block.vector
        def _(dve):
            for s in (ln.stats, ln.mv, ln.hn, tr_l, v_l, proj_l, max_ok, ptr_l, out_l, rinv_ok, added):
                s.start(dve)
            dve.wait_ge(w_hi, 1)
            dve.tensor_tensor(w0l[:, :], stage[:, 0:W3], w0h[:, :].bitcast(F32), ALU.subtract).then_inc(w_lo, 1)
            dve.wait_ge(w_hi, 2)
            dve.tensor_tensor(w1l[:, :], stage[0:D1, W3:2 * W3], w1h[0:D1, :].bitcast(F32),
                              ALU.subtract).then_inc(w_lo, 1)
            dve.wait_ge(w_hi, 3)
            dve.tensor_tensor(wol[:, :, :].rearrange("p h d -> p (h d)"), stage[:, 0:NH * D],
                              woh[:, :, :].rearrange("p h d -> p (h d)").bitcast(F32),
                              ALU.subtract).then_inc(w_lo, 1)
            dve.wait_ge(ident_ok, 5)
            with dve.Fori(0, NB) as b:
                layernorm(dve, None, h, b, hn, stats, mv, rstd, ln)
                for step in dve_steps:
                    kind = step[0]
                    if kind == "TR":
                        m = step[1]
                        src = slots[slot_of[step] % 2][:, :, :].rearrange("p a n -> p (a n)")
                        tr_h.wait(dve, b, m + 1)
                        if m == 0:
                            dve.tensor_tensor(x0l[:, :], src[:, 0:N], x0h[:, :].bitcast(F32),
                                              ALU.subtract).then_inc(tr_l.sem, 1)
                        else:
                            dve.tensor_tensor(x1s[D1:P, :], src[D1:P, 0:N], x1s[D1:P, :].bitcast(F32),
                                              ALU.subtract).then_inc(tr_l.sem, 1)
                    elif kind == "V":
                        t = step[1]
                        v_h.wait(dve, b, t + 1)
                        for a in range(2):
                            src = slots[slot_of[step] % 2][0:TQ[t], a, 0:6 * HD].rearrange("p (h n) -> p h n", n=HD)
                            hs = slice(6 * a, 6 * a + 6)
                            last = dve.tensor_tensor(v_s[0:TQ[t], t, hs, HD:2 * HD], src,
                                                     v_s[0:TQ[t], t, hs, 0:HD].bitcast(F32), ALU.subtract)
                        last.then_inc(v_l.sem, 1)
                    elif kind == "QK":
                        p, m = step[1:]
                        proj_h.wait(dve, b, 2 * p + m + 1)
                        low = (k_l[:, p % 2, :] if m else q_l[:, :]).rearrange("p (a n) -> p a n", a=2)
                        dve.scalar_tensor_tensor(low, slot_view(slot_of[step], P, HALF), (1.0 if m else 0.125),
                                                 qk_h[:, m, :].rearrange("p (a n) -> p a n", a=2).bitcast(F32),
                                                 ALU.mult, ALU.subtract).then_inc(proj_l.sem, 1)
                    elif kind == "S":
                        n, i = step[1:]
                        tq = TQ[i]
                        slot_full.wait(dve, b, slot_of[step] + 1)
                        dve.tensor_reduce(negmax[0:tq, n, i:i + 1], slot_view(slot_of[step], tq, HALF), AXXY,
                                          ALU.max, negate=True).then_inc(max_ok.sem, 1)
                    elif kind == "T":
                        n, i = step[1:]
                        ptr_h.wait(dve, b, n * 6 + i + 1)
                        for (dst, src), (high, _) in zip(transposed(pt_l, bank_of[step], i),
                                                         transposed(pt_h, bank_of[step], i)):
                            last = dve.tensor_tensor(dst, src, high.bitcast(F32), ALU.subtract)
                        last.then_inc(ptr_l.sem, 1)
                        if i == 0:
                            exp_ok.wait(dve, b, (n + 1) * NTILE)
                            dve.reciprocal(rinv[:, n, :], rowsum[:, n, :]).then_inc(rinv_ok.sem, 1)
                    elif kind == "PV" and step[2] == NTILE - 1:
                        out_h.wait(dve, b, step[1] + 1)
                        dve.tensor_tensor(o_l[:, :].rearrange("p (a n) -> p a n", a=2), o_ps[:, :, 0:HALF],
                                          o_h[:, :].rearrange("p (a n) -> p a n", a=2).bitcast(F32),
                                          ALU.subtract).then_inc(out_l.sem, 1)
                    elif kind == "Y":
                        n = step[1]
                        rinv_ok.wait(dve, b, n + 1)
                        added.wait(dve, b, 2 * n)
                        slot_full.wait(dve, b, slot_of[step] + 1)
                        for t, tq in enumerate(TQ):
                            if t < 4:
                                src = slots[slot_of[step] % 2][0:tq, t // 2, (t % 2) * D:(t % 2 + 1) * D]
                            else:
                                bank_full.wait(dve, b, bank_of[step] + 1)
                                src = banks[bank_of[step] % 2][0:tq, 0:D]
                            row = h[0:tq, bass.ds(b * NTILE + t, 1), :].rearrange("p o d -> p (o d)")
                            last = dve.scalar_tensor_tensor(row, src, rinv[0:tq, n, t:t + 1], row, ALU.mult, ALU.add)
                            if t >= 3:
                                last.then_inc(added.sem, 1)

        @block.tensor
        def _(pe):
            for s in (slot_full, bank_full, o_full):
                s.start(pe)
            pe.wait_ge(w_lo, 3)
            pe.wait_ge(ident_ok, 5)
            with pe.Fori(0, NB) as b:
                for step in steps:
                    kind = step[0]
                    if step in slot_of:
                        wait_slot_free(pe, b, slot_of[step])
                        slot = slots[slot_of[step] % 2]
                    if kind == "TR":
                        m = step[1]
                        ln.hn.wait(pe, b, 2 * NTILE)
                        flat = slot[:, :, :].rearrange("p a n -> p (a n)")
                        for t, tq in enumerate(TQ):
                            last = pe.transpose(flat[:, t * P:t * P + tq], hn[0:tq, t, m * P:(m + 1) * P],
                                                ident[0:tq, 0:tq])
                        last.then_inc(slot_full.sem, 1)
                    elif kind == "V":
                        t = step[1]
                        tr_l.wait(pe, b, 2)
                        rows = slice(t * P, t * P + TQ[t])
                        for a in range(2):
                            cols = slice(2 * NH * HD + a * 6 * HD, 2 * NH * HD + (a + 1) * 6 * HD)
                            terms = [(x0h[:, rows], w0h[:, cols]), (x0l[:, rows], w0h[:, cols]),
                                     (x0h[:, rows], w0l[:, cols]), (x1s[:, rows], w1h[:, cols]),
                                     (x1s[0:D1, rows], w1l[:, cols])]
                            for j, (lhs, rhs) in enumerate(terms):
                                last = pe.matmul(slot[0:TQ[t], a, 0:6 * HD], lhs, rhs, start=(j == 0), stop=(j == 4))
                        last.then_inc(slot_full.sem, 1)
                    elif kind == "QK":
                        p, m = step[1:]
                        cols = slice(m * NH * HD + p * P, m * NH * HD + (p + 1) * P)
                        for a in range(2):
                            rows = slice(a * HALF, (a + 1) * HALF)
                            terms = [(w0h[:, cols], x0h[:, rows]), (w0h[:, cols], x0l[:, rows]),
                                     (w0l[:, cols], x0h[:, rows]), (w1h[:, cols], x1s[:, rows]),
                                     (w1l[:, cols], x1s[0:D1, rows])]
                            for j, (lhs, rhs) in enumerate(terms):
                                last = pe.matmul(slot[:, a, 0:HALF], lhs, rhs, start=(j == 0), stop=(j == 4))
                        last.then_inc(slot_full.sem, 1)
                    elif kind == "S":
                        n, i = step[1:]
                        tq, par, e = TQ[i], n // 2 % 2, n % 2
                        if i == 0 and e == 0:
                            stacked[par].wait(pe, b, (n // 2 // 2 + 1) * 128)
                            proj_l.wait(pe, b, n + 2)
                        q = slice(i * P, i * P + tq)
                        own = slice(e * HD, (e + 1) * HD)
                        for a in range(2):
                            k = slice(a * HALF, (a + 1) * HALF)
                            pe.matmul(slot[0:tq, a, 0:HALF], q_s[:, par, e, q], k_s[:, par, e, k], start=True, stop=False)
                            last = pe.matmul(slot[0:tq, a, 0:HALF], q_s[own, par, e, q], k_l[own, par, k],
                                             start=False, stop=True)
                        last.then_inc(slot_full.sem, 1)
                    elif kind == "T":
                        n, i = step[1:]
                        k = bank_of[step]
                        wait_bank_free(pe, b, k)
                        exp_ok.wait(pe, b, (n + 1) * NTILE)
                        take_wait(pe, taken)
                        bank = banks[k % 2]
                        if i == 0:
                            for t, kw in enumerate(TQ):
                                last = pe.transpose(bank[0:kw, t * NT:(t + 1) * NT],
                                                    prob[0:NT, n % 2, 4, t * P:t * P + kw], ident[0:NT, 0:NT])
                        else:
                            kw = TQ[i - 1]
                            for t in range(4):
                                last = pe.transpose(bank[0:kw, t * P:(t + 1) * P],
                                                    prob[:, n % 2, t, (i - 1) * P:(i - 1) * P + kw], ident[:, :])
                        last.then_inc(bank_full.sem, 1)
                    elif kind == "PV":
                        n, t = step[1:]
                        ptr_l.wait(pe, b, n * 6 + t + 2)
                        if t == 0:
                            v_l.wait(pe, b, NTILE)
                            out_l.wait(pe, b, n)
                        kw = TQ[t]
                        for a in range(2):
                            q = slice(a * HALF, (a + 1) * HALF)
                            pe.matmul(o_ps[:, a, 0:HALF], v_s[0:kw, t, n, :], pt_h[0:kw, t, q],
                                      start=(t == 0), stop=False)
                            last = pe.matmul(o_ps[:, a, 0:HALF], v_s[0:kw, t, n, :], pt_l[0:kw, t, q],
                                             start=False, stop=(t == NTILE - 1))
                        if t == NTILE - 1:
                            last.then_inc(o_full.sem, 1)
                    elif kind == "Y":
                        n = step[1]
                        out_l.wait(pe, b, n + 1)
                        for t, tq in enumerate(TQ):
                            if t < 4:
                                dst = slot[0:tq, t // 2, (t % 2) * D:(t % 2 + 1) * D]
                            else:
                                wait_bank_free(pe, b, bank_of[step])
                                dst = banks[bank_of[step] % 2][0:tq, 0:D]
                            rows = slice(t * P, t * P + tq)
                            for j, (lhs, rhs) in enumerate(((o_h, woh), (o_l, woh), (o_h, wol))):
                                last = pe.matmul(dst, lhs[:, rows], rhs[:, n, :], start=(j == 0), stop=(j == 2))
                            if t == 3:
                                last.then_inc(slot_full.sem, 1)
                        last.then_inc(bank_full.sem, 1)


def ffn_phase(nc, sem, h, aps):
    phi0_d, phi1_d, w1a_d, w1b_d, b1_d, w2_d, b2_d, out_d = aps
    order = [("TR", 0), ("TR", 1)] + [("L", t) for t in range(NTILE)] + [("LT", m) for m in range(NM)]
    order += [("CT", m) for m in range(NM)] + [("DT", t) for t in range(NTILE)] + [("SL", 0), ("SL", 1)]
    order += [("H", 0, 0), ("H", 0, 1)]
    for e in range(1, NE):
        order += [("H", e, 0), ("H", e, 1), ("Y", e - 1)]
    order += [("Y", NE - 1)] + [("O", t) for t in range(NTILE)]
    NU = len(order)
    at = {u: i for i, u in enumerate(order)}
    NSLOTS = 4
    with ExitStack() as ctx:
        def sb(name, shape, dt=F32):
            return ctx.enter_context(nc.sbuf_tensor(name, shape, dt))
        ident = sb("ff_ident", [P, P])
        hn = sb("ff_hn", [P, NTILE, D])
        stats = sb("ff_stats", [P, NTILE, 6])
        mv = sb("ff_mv", [P, NTILE, 2])
        rstd = sb("ff_rstd", [P, 3, NTILE])
        phi0, phi1 = sb("ff_phi0", [P, ES]), sb("ff_phi1", [D1, ES])
        w1a, w1b = sb("ff_w1a", [P, NE, FH]), sb("ff_w1b", [D1, NE, FH])
        b1, b2 = sb("ff_b1", [P, NE * FM]), sb("ff_b2", [P, NE, D])
        w2 = sb("ff_w2", [P, NE, FM, D])
        x0, x1 = sb("ff_x0", [P, N]), sb("ff_x1", [D1, N])
        logit = sb("ff_logit", [P, NTILE, ES])
        comb = sb("ff_comb", [P, NTILE, ES])
        disp = sb("ff_disp", [P, NM, N])
        comb_t = sb("ff_comb_t", [P, NM, N])
        s0, s1 = sb("ff_s0", [P, ES]), sb("ff_s1", [D1, ES])
        hid = sb("ff_hid", [P, 2, FM, NS])
        y = sb("ff_y", [P, NM, D])
        fin = sb("ff_fin", [P, NTILE, D])
        nmc, sumc, rc = (sb(n, [P, NTILE]) for n in ("ff_nmc", "ff_sumc", "ff_rc"))
        nmd, sumd, rd = (sb(n, [P, NM]) for n in ("ff_nmd", "ff_sumd", "ff_rd"))
        slots = [ctx.enter_context(nc.psum_tensor(f"ff_slot{i}", [P, 1024], F32)) for i in range(NSLOTS)]

        w_in = sem("ff_w_in")
        const_ok = sem("ff_const")
        taken = sem("ff_taken")
        ln = LnSems(sem, "ff_ln", NTILE)
        full = Tally(sem("ff_full"), NU)
        tr_out = Tally(sem("ff_tr_out"), 2)
        maxc = Tally(sem("ff_maxc"), NTILE)
        logit_out = Tally(sem("ff_logit_out"), NTILE)
        comb_ok = Tally(sem("ff_comb_ok"), NTILE)
        rc_ok = Tally(sem("ff_rc_ok"), 1)
        maxd = Tally(sem("ff_maxd"), NM)
        disp_exp = Tally(sem("ff_disp_exp"), NM)
        rd_ok = Tally(sem("ff_rd_ok"), NM)
        disp_ok = Tally(sem("ff_disp_ok"), NM)
        ct_out = Tally(sem("ff_ct_out"), NM)
        dt_out = Tally(sem("ff_dt_out"), NTILE)
        sl_out = Tally(sem("ff_sl_out"), 2)
        hid_ok = Tally(sem("ff_hid_ok"), 2 * NE)
        y_ok = Tally(sem("ff_y_ok"), NE)
        fin_ok = Tally(sem("ff_fin_ok"), NTILE)
        sent = Tally(sem("ff_sent"), 32)
        block = ctx.enter_context(nc.Block())

        def normalise(dve, b, m):
            disp_exp.wait(dve, b, m + 1)
            dve.reciprocal(rd[:, m:m + 1], sumd[:, m:m + 1]).then_inc(rd_ok.sem, 1)
            rd_ok.wait(dve, b, m + 1)
            dve.tensor_scalar(disp[:, m, :], disp[:, m, :], rd[:, m:m + 1], None, ALU.mult).then_inc(disp_ok.sem, 1)

        def released(u):
            return {
                "TR": lambda: (tr_out, u[1] + 1),
                "L": lambda: (logit_out, u[1] + 1),
                "LT": lambda: (disp_exp, u[1] + 1),
                "CT": lambda: (ct_out, u[1] + 1),
                "DT": lambda: (dt_out, u[1] + 1),
                "SL": lambda: (sl_out, u[1] + 1),
                "H": lambda: (hid_ok, 2 * u[1] + u[2] + 1),
                "Y": lambda: (y_ok, u[1] + 1),
                "O": lambda: (fin_ok, u[1] + 1),
            }[u[0]]()

        def slot(u):
            return slots[at[u] % NSLOTS]

        def slot_free(eng, b, u):
            k, back = at[u], 1
            while (k - back) % NU % NSLOTS != k % NSLOTS:
                back += 1
            unit = order[(k - back) % NU]
            if (u[0], unit[0]) in (("L", "TR"), ("LT", "L"), ("SL", "DT"), ("H", "SL"), ("Y", "H"), ("O", "Y")):
                return
            tally, count = released(unit)
            tally.wait(eng, b, count - (tally.per if k < back else 0))

        @block.sync
        def _(sp):
            sent.start(sp)
            for dst, src in ((phi0, phi0_d), (phi1, phi1_d), (w1a, w1a_d), (w1b, w1b_d), (b1, b1_d),
                             (b2, b2_d), (w2, w2_d)):
                flat = dst[:]
                if len(dst.shape) == 3:
                    flat = dst[:, :, :].rearrange("p a b -> p (a b)")
                elif len(dst.shape) == 4:
                    flat = dst[:, :, :, :].rearrange("p a b c -> p (a b c)")
                sp.dma_start(flat, src).then_inc(w_in, 16)
            with sp.Fori(0, NB) as b:
                main = out_d[bass.ds(b, 1), 0:NX, :].rearrange("o (t p) d -> p (o t) d", p=P)
                tail = out_d[bass.ds(b, 1), NX:N, :].rearrange("o n d -> (o n) d")
                fin_ok.wait(sp, b, NTILE)
                sp.dma_start(main, fin[:, 0:4, :]).then_inc(sent.sem, 16)
                sp.dma_start(tail, fin[0:NT, 4, :]).then_inc(sent.sem, 16)
            sp.wait_ge(sent.sem, (NB + 1) * 32)

        @block.gpsimd
        def _(pool):
            ln.rstd.start(pool)
            pool.memset(ident[:, :], 0.0).then_inc(const_ok, 1)
            pool.memset(rstd[:, :, :], -0.5).then_inc(const_ok, 1)
            pool.memset(mv[:, :, :], 1.0).then_inc(const_ok, 1)
            pool.memset(sumc[:, :], 1.0).then_inc(const_ok, 1)
            pool.wait_ge(const_ok, 4)
            pool.affine_select(out=ident[:, :], in_=ident[:, :], compare_op=ALU.not_equal, fill=1.0, base=0,
                               pattern=[[-1, P]], channel_multiplier=1).then_inc(const_ok, 1)
            with pool.Fori(0, NB) as b:
                layernorm(None, pool, h, b, hn, stats, mv, rstd, ln)

        @block.scalar
        def _(act):
            for s in (comb_ok, disp_exp, dt_out, hid_ok):
                s.start(act)
            act.wait_ge(const_ok, 5)
            act.wait_ge(w_in, 7 * 16)
            with act.Fori(0, NB) as b:
                for u in order:
                    kind = u[0]
                    if kind == "L":
                        t, tq = u[1], TQ[u[1]]
                        logit_out.wait(act, b, t + 1)
                        act.activation(comb[0:tq, t, :], logit[0:tq, t, :], ACT.Exp, bias=nmc[0:tq, t:t + 1],
                                       accum_out=sumc[0:tq, t:t + 1]).then_inc(comb_ok.sem, 1)
                    elif kind == "LT":
                        m = u[1]
                        maxd.wait(act, b, m + 1)
                        act.activation(disp[:, m, :], slot(u)[:, 0:N], ACT.Exp, bias=nmd[:, m:m + 1],
                                       accum_out=sumd[:, m:m + 1]).then_inc(disp_exp.sem, 1)
                    elif kind == "DT":
                        t, tq = u[1], TQ[u[1]]
                        full.wait(act, b, at[u] + 1)
                        act.activation(logit[0:tq, t, :], slot(u)[0:tq, :], ACT.Copy).then_inc(dt_out.sem, 1)
                    elif kind == "H":
                        e, part = u[1:]
                        full.wait(act, b, at[u] + 1)
                        ms = range(4) if part == 0 else range(4, FM)
                        for m in ms:
                            last = act.activation(hid[:, e % 2, m, :], slot(u)[:, (m - ms[0]) * NS:(m - ms[0] + 1) * NS],
                                                  ACT.Gelu_apprx_tanh, bias=b1[:, e * FM + m:e * FM + m + 1])
                        last.then_inc(hid_ok.sem, 1)

        @block.vector
        def _(dve):
            for s in (ln.stats, ln.mv, ln.hn, tr_out, maxc, logit_out, rc_ok, maxd, rd_ok, disp_ok, ct_out,
                      sl_out, y_ok, fin_ok):
                s.start(dve)
            dve.wait_ge(const_ok, 5)
            dve.wait_ge(w_in, 7 * 16)
            with dve.Fori(0, NB) as b:
                layernorm(dve, None, h, b, hn, stats, mv, rstd, ln)
                for u in order:
                    kind = u[0]
                    if kind == "TR":
                        full.wait(dve, b, at[u] + 1)
                        dst = x1[:, :] if u[1] else x0[:, :]
                        dve.tensor_copy(dst, slot(u)[0:dst.shape[0], 0:N]).then_inc(tr_out.sem, 1)
                    elif kind == "L":
                        t, tq = u[1], TQ[u[1]]
                        full.wait(dve, b, at[u] + 1)
                        dve.tensor_reduce(nmc[0:tq, t:t + 1], slot(u)[0:tq, :], AXX, ALU.max,
                                          negate=True).then_inc(maxc.sem, 1)
                        dve.tensor_copy(logit[0:tq, t, :], slot(u)[0:tq, :]).then_inc(logit_out.sem, 1)
                    elif kind == "LT":
                        m = u[1]
                        full.wait(dve, b, at[u] + 1)
                        dve.tensor_reduce(nmd[:, m:m + 1], slot(u)[:, 0:N], AXX, ALU.max,
                                          negate=True).then_inc(maxd.sem, 1)
                        if m >= 1:
                            normalise(dve, b, m - 1)
                    elif kind == "CT":
                        m = u[1]
                        if m == 0:
                            normalise(dve, b, NM - 1)
                        full.wait(dve, b, at[u] + 1)
                        dve.tensor_copy(comb_t[:, m, :], slot(u)[:, 0:N]).then_inc(ct_out.sem, 1)
                    elif kind == "SL":
                        full.wait(dve, b, at[u] + 1)
                        dst = s1[:, :] if u[1] else s0[:, :]
                        dve.tensor_copy(dst, slot(u)[0:dst.shape[0], :]).then_inc(sl_out.sem, 1)
                    elif kind == "Y":
                        e = u[1]
                        full.wait(dve, b, at[u] + 1)
                        for st in range(2):
                            last = dve.tensor_tensor(y[:, 2 * e + st, :], slot(u)[:, st * D:(st + 1) * D],
                                                     b2[:, e, :], ALU.add)
                        last.then_inc(y_ok.sem, 1)
                    elif kind == "O":
                        t, tq = u[1], TQ[u[1]]
                        if t == 0:
                            comb_ok.wait(dve, b, NTILE)
                            dve.reciprocal(rc[:, :], sumc[:, :]).then_inc(rc_ok.sem, 1)
                            sent.wait(dve, b, 0)
                            rc_ok.wait(dve, b, 1)
                        full.wait(dve, b, at[u] + 1)
                        row = h[0:tq, bass.ds(b * NTILE + t, 1), :].rearrange("p o d -> p (o d)")
                        dve.scalar_tensor_tensor(fin[0:tq, t, :], slot(u)[0:tq, 0:D], rc[0:tq, t:t + 1], row,
                                                 ALU.mult, ALU.add).then_inc(fin_ok.sem, 1)

        @block.tensor
        def _(pe):
            full.start(pe)
            pe.wait_ge(const_ok, 5)
            pe.wait_ge(w_in, 7 * 16)
            with pe.Fori(0, NB) as b:
                for u in order:
                    kind = u[0]
                    slot_free(pe, b, u)
                    out = slot(u)
                    if kind == "TR":
                        m = u[1]
                        ln.hn.wait(pe, b, NTILE)
                        take_wait(pe, taken)
                        for t, tq in enumerate(TQ):
                            w = P if m == 0 else D1
                            last = pe.transpose(out[0:w, t * P:t * P + tq], hn[0:tq, t, m * P:m * P + w],
                                                ident[0:tq, 0:tq])
                    elif kind == "L":
                        t, tq = u[1], TQ[u[1]]
                        tr_out.wait(pe, b, 2)
                        for a in range(2):
                            cols = slice(a * 512, (a + 1) * 512)
                            pe.matmul(out[0:tq, cols], x0[:, t * P:t * P + tq], phi0[:, cols], start=True, stop=False)
                            last = pe.matmul(out[0:tq, cols], x1[:, t * P:t * P + tq], phi1[:, cols],
                                             start=False, stop=True)
                    elif kind == "LT":
                        logit_out.wait(pe, b, NTILE)
                        take_wait(pe, taken)
                        for t, tq in enumerate(TQ):
                            last = pe.transpose(out[:, t * P:t * P + tq], logit[0:tq, t, u[1] * P:(u[1] + 1) * P],
                                                ident[0:tq, 0:tq])
                    elif kind == "CT":
                        comb_ok.wait(pe, b, NTILE)
                        take_wait(pe, taken)
                        for t, tq in enumerate(TQ):
                            last = pe.transpose(out[:, t * P:t * P + tq], comb[0:tq, t, u[1] * P:(u[1] + 1) * P],
                                                ident[0:tq, 0:tq])
                    elif kind == "DT":
                        t, tq = u[1], TQ[u[1]]
                        disp_ok.wait(pe, b, NM)
                        take_wait(pe, taken)
                        for m in range(NM):
                            last = pe.transpose(out[0:tq, m * P:(m + 1) * P], disp[:, m, t * P:t * P + tq],
                                                ident[:, :])
                    elif kind == "SL":
                        w = D1 if u[1] else P
                        dt_out.wait(pe, b, NTILE)
                        for a in range(2):
                            cols = slice(a * 512, (a + 1) * 512)
                            for t, tq in enumerate(TQ):
                                last = pe.matmul(out[0:w, cols], hn[0:tq, t, u[1] * P:u[1] * P + w],
                                                 logit[0:tq, t, cols], start=(t == 0), stop=(t == NTILE - 1))
                    elif kind == "H":
                        e, part = u[1:]
                        sl_out.wait(pe, b, 2)
                        ms = range(4) if part == 0 else range(4, FM)
                        for m in ms:
                            dst = out[:, (m - ms[0]) * NS:(m - ms[0] + 1) * NS]
                            pe.matmul(dst, w1a[:, e, m * P:(m + 1) * P], s0[:, e * NS:(e + 1) * NS],
                                      start=True, stop=False)
                            last = pe.matmul(dst, w1b[:, e, m * P:(m + 1) * P], s1[:, e * NS:(e + 1) * NS],
                                             start=False, stop=True)
                    elif kind == "Y":
                        e = u[1]
                        hid_ok.wait(pe, b, 2 * e + 2)
                        for st in range(2):
                            for m in range(FM):
                                last = pe.matmul(out[:, st * D:(st + 1) * D], hid[:, e % 2, m, st * P:(st + 1) * P],
                                                 w2[:, e, m, :], start=(m == 0), stop=(m == FM - 1))
                    elif kind == "O":
                        t, tq = u[1], TQ[u[1]]
                        ct_out.wait(pe, b, NM)
                        y_ok.wait(pe, b, NE)
                        for m in range(NM):
                            last = pe.matmul(out[0:tq, 0:D], comb_t[:, m, t * P:t * P + tq], y[:, m, :],
                                             start=(m == 0), stop=(m == NM - 1))
                    last.then_inc(full.sem, 1)


def early_fusion_kernel(nc, x_d, txt_d, f_d, wtok_d, w0_d, w1_d, wo_d,
                        phi0_d, phi1_d, w1a_d, w1b_d, b1_d, w2_d, b2_d, out_d):
    with ExitStack() as ctx:
        def sem(name):
            return ctx.enter_context(nc.semaphore(name))
        h = ctx.enter_context(nc.sbuf_tensor("h", [P, NB * NTILE, D], F32))
        tok_phase(nc, sem, h, (x_d, wtok_d, f_d, txt_d))
        attn_phase(nc, sem, h, (w0_d, w1_d, wo_d))
        ffn_phase(nc, sem, h, (phi0_d, phi1_d, w1a_d, w1b_d, b1_d, w2_d, b2_d, out_d))


def laid_out(x, txt, freq, w_tok, w_qkv, w_o, phi, w1, b1, w2, b2):
    import numpy as np
    c = np.ascontiguousarray
    xt = x.reshape(NB, NX, 3 * D).transpose(0, 2, 1)
    full = (CH - 1) * P
    x_l = np.concatenate([xt[:, :full].reshape(NB, CH - 1, P, NX),
                          np.concatenate([xt[:, full:], xt[:, full:]], 1)[:, None]], 1)
    wt = w_tok.reshape(D, 3 * D, 2, BANDS).transpose(2, 3, 1, 0)
    units = [wt[kind, 2 * jp + jj, ch * P:(ch + 1) * P]
             for ch in range(CH - 1) for jp in range(3) for kind in range(2) for jj in range(2)]
    units += [np.concatenate([wt[0, j, full:], wt[1, j, full:]]) for j in range(BANDS)]
    qkv = w_qkv.transpose(2, 1, 0, 3).reshape(D, 3 * NH * HD)
    wo = w_o.reshape(NH, HD, D).transpose(1, 0, 2).reshape(HD, NH * D)
    phi_t = phi.reshape(ES, D).T
    w1_t = w1.transpose(1, 0, 2).reshape(D, NE * FH)
    return {
        "x": c(x_l), "txt": c(txt), "freq": c(np.broadcast_to(freq, (P, BANDS))),
        "w_tok": c(np.stack(units, 1).reshape(P, NKU * D)),
        "w_qkv0": c(qkv[:P]), "w_qkv1": c(np.concatenate([qkv[P:], qkv[P:]])), "w_o": c(np.concatenate([wo, wo])),
        "phi0": c(phi_t[:P]), "phi1": c(phi_t[P:]), "w1a": c(w1_t[:P]), "w1b": c(w1_t[P:]),
        "b1": c(b1.reshape(NE * FM, P).T),
        "w2": c(w2.reshape(NE, FM, P, D).transpose(2, 0, 1, 3).reshape(P, NE * FM * D)),
        "b2": c(np.broadcast_to(b2.reshape(1, NE * D), (P, NE * D))),
    }


def kernel(x, txt, L0_tok_freq_bands, L0_tok_W, L0_attn_w_qkv, L0_attn_w_o, L0_ffn_phi, L0_ffn_w1,
           L0_ffn_b1, L0_ffn_w2, L0_ffn_b2):
    import numpy as np
    import concourse.bacc as bacc
    from concourse.bass_utils import run_bass_kernel_spmd

    given = [np.asarray(a) for a in (x, txt, L0_tok_freq_bands, L0_tok_W, L0_attn_w_qkv, L0_attn_w_o, L0_ffn_phi,
                                     L0_ffn_w1, L0_ffn_b1, L0_ffn_w2, L0_ffn_b2)]
    nc = bacc.Bacc("TRN2", target_bir_lowering=False, num_devices=1)
    arrays, args = {}, []
    for name, a in laid_out(*given).items():
        arrays[f"in_{name}_dram"] = a
        args.append(nc.dram_tensor(f"in_{name}_dram", a.shape, mybir.dt.from_np(a.dtype), kind="ExternalInput").ap())
    args.append(nc.dram_tensor("out_0_dram", (NB, N, D), F32, kind="ExternalOutput").ap())
    early_fusion_kernel(nc, *args)
    r = run_bass_kernel_spmd(nc, [arrays], core_ids=[0])
    return r.results[0]["out_0_dram"]
```

```python
from contextlib import ExitStack

import concourse.bass as bass
from concourse import mybir

F32 = mybir.dt.float32
F32R = mybir.dt.float32r
ACT = mybir.ActivationFunctionType
ALU = mybir.AluOpType
AXX = mybir.AxisListType.X
AXXY = mybir.AxisListType.XY

P = 128
NB, NX, NT, D = 8, 512, 32, 192
N = NX + NT
TQ = [128, 128, 128, 128, 32]
NTILE = len(TQ)
HALF = N // 2
D1 = D - P
BANDS = 6
CH = 5
NKU = (CH - 1) * 2 * BANDS + BANDS
EPS = 1e-5
MAGIC = 12582912.0
TWO_PI = 6.2831845
HALF_PI = 1.5707963

NH, HD = 12, 64
NP = NH // 2
NE, NS, FH = 4, 256, 768
ES = NE * NS
NM = ES // P
FM = FH // P


class Tally:

    def __init__(self, sem, per):
        self.sem, self.per = sem, per

    def start(self, eng, ahead=0):
        if self.per > ahead:
            eng.sem_inc(self.sem, self.per - ahead)

    def wait(self, eng, it, k):
        eng.wait_ge(self.sem, it * self.per + (self.per + k))


def tok_phase(nc, sem, h, aps):
    x_d, w_d, f_d, txt_d = aps
    NU = CH * 3
    SLOTS = 3
    made = [0]
    for u in range(NU):
        made.append(made[-1] + (2 if u // 3 < CH - 1 else 1))
    with ExitStack() as ctx:
        def sb(name, shape, dt=F32):
            return ctx.enter_context(nc.sbuf_tensor(name, shape, dt))
        w = sb("tok_w", [P, NKU, D])
        freq = sb("tok_freq", [P, BANDS])
        x = sb("tok_x", [P, CH, NX])
        shifted = sb("tok_shifted", [P, 2, NX])
        whole = sb("tok_whole", [P, 2, NX])
        turn = sb("tok_turn", [P, SLOTS, 2, NX])
        absturn = sb("tok_absturn", [P, SLOTS, 2, NX])
        feat = sb("tok_feat", [P, SLOTS, 2, 2, NX])
        sc = sb("tok_sc", [P, 3])
        acc = [ctx.enter_context(nc.psum_tensor(f"tok_acc{t}", [P, 512], F32)) for t in range(4)]

        w_in = sem("tok_w_in")
        f_in = sem("tok_f_in")
        txt_in = sem("tok_txt_in")
        const_ok = sem("tok_const_ok")
        x_in = [Tally(sem(f"tok_x_in{c}"), 16) for c in range(CH)]
        x_used = Tally(sem("tok_x_used"), CH)
        shifted_ok = Tally(sem("tok_shifted_ok"), 2 * NU)
        whole_ok = Tally(sem("tok_whole_ok"), NU)
        turn_ok = Tally(sem("tok_turn_ok"), 2 * NU)
        abs_ok = Tally(sem("tok_abs_ok"), NU)
        feat_ok = Tally(sem("tok_feat_ok"), made[-1])
        feat_used = Tally(sem("tok_feat_used"), NU)
        acc_ok = Tally(sem("tok_acc_ok"), 3)
        acc_out = Tally(sem("tok_acc_out"), 4)
        block = ctx.enter_context(nc.Block())

        @block.sync
        def _(sp):
            for c in range(CH):
                x_in[c].start(sp)
            sp.dma_start(freq[:, :], f_d).then_inc(f_in, 16)
            for c in range(CH):
                sp.dma_start(x[:, c, :], x_d[0, c]).then_inc(x_in[c].sem, 16)
            sp.dma_start(w[:, :, :].rearrange("p k n -> p (k n)"), w_d).then_inc(w_in, 16)
            sp.dma_start(h[0:NT, NTILE - 1:NB * NTILE:NTILE, :],
                         txt_d.rearrange("b n d -> n b d")).then_inc(txt_in, 16)
            with sp.Fori(0, NB - 1) as b:
                for c in range(CH):
                    src = x_d[bass.ds(b + 1, 1), c].rearrange("o p n -> (o p) n")
                    x_used.wait(sp, b, c + 1)
                    sp.dma_start(x[:, c, :], src).then_inc(x_in[c].sem, 16)
            sp.wait_ge(w_in, 16)
            sp.wait_ge(txt_in, 16)

        @block.vector
        def _(dve):
            for s in (x_used, shifted_ok, whole_ok, turn_ok, abs_ok):
                s.start(dve)
            dve.memset(sc[0:D1, 0:1], TWO_PI)
            dve.memset(sc[D1:P, 0:1], -TWO_PI)
            dve.memset(sc[0:D1, 1:2], 0.0)
            dve.memset(sc[D1:P, 1:2], HALF_PI)
            dve.memset(sc[:, 2:3], HALF_PI).then_inc(const_ok, 1)
            dve.wait_ge(f_in, 16)
            with dve.Fori(0, NB) as b:
                for u in range(NU):
                    c, jp, s = u // 3, u % 3, u % SLOTS
                    if jp == 0:
                        x_in[c].wait(dve, b, 16)
                    turn_ok.wait(dve, b, 2 * u)
                    for jj in range(2):
                        j = 2 * jp + jj
                        dve.tensor_scalar(shifted[:, jj, :], x[:, c, :], freq[:, j:j + 1], MAGIC,
                                          ALU.mult, ALU.add).then_inc(shifted_ok.sem, 1)
                    shifted_ok.wait(dve, b, 2 * u + 2)
                    dve.tensor_scalar(whole[:, :, :], shifted[:, :, :], MAGIC, None,
                                      ALU.subtract).then_inc(whole_ok.sem, 1)
                    whole_ok.wait(dve, b, u + 1)
                    prev = u - SLOTS
                    feat_ok.wait(dve, b, made[prev + 1] if prev >= 0 else made[prev + NU + 1] - made[-1])
                    for jj in range(2):
                        j = 2 * jp + jj
                        dve.scalar_tensor_tensor(turn[:, s, jj, :], x[:, c, :], freq[:, j:j + 1],
                                                 whole[:, jj, :], ALU.mult,
                                                 ALU.subtract).then_inc(turn_ok.sem, 1)
                    turn_ok.wait(dve, b, 2 * u + 2)
                    if c < CH - 1:
                        dve.scalar_tensor_tensor(absturn[:, s, :, :], turn[:, s, :, :], -1.0, turn[:, s, :, :],
                                                 ALU.mult, ALU.max).then_inc(abs_ok.sem, 1)
                    else:
                        dve.scalar_tensor_tensor(turn[D1:P, s, :, :], turn[D1:P, s, :, :], -1.0,
                                                 turn[D1:P, s, :, :], ALU.mult,
                                                 ALU.max).then_inc(abs_ok.sem, 1)
                    if jp == 2:
                        dve.sem_inc(x_used.sem, 1)

        @block.scalar
        def _(act):
            feat_ok.start(act)
            acc_out.start(act)
            act.wait_ge(const_ok, 1)
            with act.Fori(0, NB) as b:
                for u in range(NU):
                    c, s = u // 3, u % SLOTS
                    feat_used.wait(act, b, u - SLOTS + 1)
                    if c < CH - 1:
                        turn_ok.wait(act, b, 2 * u + 2)
                        act.activation(feat[:, s, 0, :, :], turn[:, s, :, :], ACT.Sin,
                                       scale=TWO_PI).then_inc(feat_ok.sem, 1)
                        abs_ok.wait(act, b, u + 1)
                        act.activation(feat[:, s, 1, :, :], absturn[:, s, :, :], ACT.Sin, bias=sc[:, 2:3],
                                       scale=-TWO_PI).then_inc(feat_ok.sem, 1)
                    else:
                        abs_ok.wait(act, b, u + 1)
                        act.activation(feat[:, s, 0, :, :], turn[:, s, :, :], ACT.Sin, bias=sc[:, 1:2],
                                       scale=sc[:, 0:1]).then_inc(feat_ok.sem, 1)
                for t in range(4):
                    if t < 3:
                        acc_ok.wait(act, b, t + 1)
                    else:
                        feat_used.wait(act, b, NU)
                    act.activation(h[:, bass.ds(b * NTILE + t, 1), :].rearrange("p o d -> p (o d)"),
                                   acc[t][:, 0:D], ACT.Copy).then_inc(acc_out.sem, 1)

        @block.tensor
        def _(pe):
            feat_used.start(pe)
            acc_ok.start(pe)
            pe.wait_ge(w_in, 16)
            with pe.Fori(0, NB) as b:
                k = 0
                for u in range(NU):
                    c, s = u // 3, u % SLOTS
                    for kind in range(2 if c < CH - 1 else 1):
                        feat_ok.wait(pe, b, made[u] + kind + 1)
                        for jj in range(2):
                            for t in range(4):
                                if k == 0:
                                    acc_out.wait(pe, b, t - 3)
                                last = pe.matmul(acc[t][:, 0:D], feat[:, s, kind, jj, t * P:(t + 1) * P],
                                                 w[:, k, :], start=(k == 0), stop=(k == NKU - 1))
                                if k == NKU - 1 and t < 3:
                                    last.then_inc(acc_ok.sem, 1)
                            k += 1
                    last.then_inc(feat_used.sem, 1)



def rows_of(h, batch, t, c0=0, c1=D):
    rows = h[0:TQ[t], bass.ds(batch * NTILE + t, 1), c0:c1]
    return rows.rearrange("p o d -> p (o d)")


class LayerNorm:

    def __init__(self, sem, name, h, hn, stats, mv, rstd):
        self.h, self.hn, self.stats, self.mv, self.rstd = h, hn, stats, mv, rstd
        self.pieces = [(0, D, 0)] + ([(P, D, D)] if hn.shape[2] > D else [])
        self.stats_ok = Tally(sem(name + "_stats"), NTILE)
        self.mv_ok = Tally(sem(name + "_mv"), NTILE)
        self.rstd_ok = Tally(sem(name + "_rstd"), 2)
        self.hn_ok = Tally(sem(name + "_hn"), NTILE)
        self.taken = sem(name + "_taken")

    def start(self, dve, ahead):
        for s in (self.stats_ok, self.mv_ok, self.hn_ok):
            s.start(dve, s.per if ahead else 0)

    def sums(self, dve, batch, t):
        dve.bn_stats(self.stats[0:TQ[t], t, :], rows_of(self.h, batch, t)).then_inc(self.stats_ok.sem, 1)

    def moments(self, dve, it, t):
        self.stats_ok.wait(dve, it, t + 1)
        take_wait(dve, self.taken)
        dve.bn_aggr(self.mv[0:TQ[t], t, :], self.stats[0:TQ[t], t, :]).then_inc(self.mv_ok.sem, 1)

    def scale(self, pool, it):
        self.mv_ok.wait(pool, it, NTILE)
        take_wait(pool, self.taken)
        pool.tensor_scalar(self.rstd[:, 0, :], self.mv[:, :, 1], EPS, None, ALU.add).then_inc(self.rstd_ok.sem, 1)
        self.rstd_ok.wait(pool, it, 1)
        pool.tensor_tensor(self.rstd[:, 1, :], self.rstd[:, 0, :], self.rstd[:, 2, :],
                           ALU.pow).then_inc(self.rstd_ok.sem, 1)

    def apply(self, dve, it, batch, t):
        self.rstd_ok.wait(dve, it, 2)
        for c0, c1, o in self.pieces:
            last = dve.tensor_scalar(self.hn[0:TQ[t], t, o:o + c1 - c0], rows_of(self.h, batch, t, c0, c1),
                                     self.mv[0:TQ[t], t, 0:1], self.rstd[0:TQ[t], 1, t:t + 1],
                                     ALU.subtract, ALU.mult)
        last.then_inc(self.hn_ok.sem, 1)

    def whole(self, dve, it, batch):
        for t in range(NTILE):
            self.sums(dve, batch, t)
        for t in range(NTILE):
            self.moments(dve, it, t)
        for t in range(NTILE):
            self.apply(dve, it, batch, t)


def ahead(it):
    return isinstance(it, int)


def take_wait(eng, taken):
    eng.sem_inc(taken, 1)


def attn_order():
    steps = []
    for n in range(NH + 2):
        old, older = 0 <= n - 1 < NH, 0 <= n - 2 < NH
        for i in range(NTILE):
            if i == 1 and older:
                steps.append(("PV", n - 2, 4))
            if n < NH:
                steps.append(("S", n, i))
            if n == 0:
                steps.append(("V", i))
            if old:
                steps += [("T", n - 1, u) for u in {0: [], 1: [0, 1], 2: [2], 3: [3], 4: [4, 5]}[i]]
            if i == 0 and older:
                steps += [("PV", n - 2, 2), ("PV", n - 2, 3)]
            if i >= 3 and old:
                steps.append(("PV", n - 1, i - 3))
            if i == (0 if n % 2 else 2) and n // 2 + 1 < NP:
                steps.append(("QK", n // 2 + 1, n % 2))
            if i in (2, 3) and n == 10:
                steps.append(("TR", i - 2))
            if i in (2, 3) and n == 11:
                steps.append(("QK", 0, i - 2))
            if i == 3 and older:
                steps.append(("Y", n - 2))
            if n in (6, 7, 8):
                steps.append((("LS", "LM", "LA")[n - 6], i))
    return steps


def swapped(steps, first, second):
    out, at = [], None
    for s in steps:
        if s[0] == first and at is not None:
            out.insert(at, s)
            at += 1
        else:
            out.append(s)
            at = len(out) - 1 if s[0] == second else None
    return out


def attn_phase(nc, sem, h, aps):
    w0_d, w1_d, wo_d = aps
    W3 = 3 * NH * HD
    steps = attn_order()
    slot_of = {s: i for i, s in enumerate(x for x in steps if x[0] in ("TR", "QK", "S", "Y"))}
    bank_of = {s: i for i, s in enumerate(x for x in steps if x[0] in ("T", "Y"))}
    slot_users = list(slot_of)
    act_steps = swapped(steps, "T", "S")
    PRO = [("TR", 0), ("TR", 1), ("QK", 0, 0), ("QK", 0, 1)]
    qk_index = {s: i for i, s in enumerate(x for x in steps if x[0] == "QK")}
    NSLOT, NBANK = len(slot_of), len(bank_of)
    with ExitStack() as ctx:
        def sb(name, shape, dt=F32):
            return ctx.enter_context(nc.sbuf_tensor(name, shape, dt))

        def ps(name, shape):
            return ctx.enter_context(nc.psum_tensor(name, shape, F32))
        ident = sb("at_ident", [P, P])
        hn = sb("at_hn", [P, NTILE, 2 * P])
        stats = sb("at_stats", [P, NTILE, 6])
        mv = sb("at_mv", [P, NTILE, 2])
        rstd = sb("at_rstd", [P, 3, NTILE])
        x0h, x0l, x1s = (sb(n, [P, N], F32R) for n in ("at_x0h", "at_x0l", "at_x1s"))
        w0h, w0l, w1h = (sb(n, [P, W3], F32R) for n in ("at_w0h", "at_w0l", "at_w1h"))
        w1l = sb("at_w1l", [D1, W3], F32R)
        woh, wol = (sb(n, [P, NH, D], F32R) for n in ("at_woh", "at_wol"))
        qk_h = sb("at_qk_h", [P, 2, N], F32R)
        q_l = sb("at_q_l", [P, N], F32R)
        k_l = sb("at_k_l", [P, 2, N], F32R)
        q_s = sb("at_q_s", [P, 2, 2, N], F32R)
        k_s = sb("at_k_s", [P, 2, 2, N], F32R)
        v_s = sb("at_v_s", [P, NTILE, NH, 2 * HD], F32R)
        prob = sb("at_prob", [P, 2, NTILE, N])
        pt_h, pt_l = (sb(n, [P, NTILE, N], F32R) for n in ("at_pt_h", "at_pt_l"))
        o_h, o_l = (sb(n, [P, N], F32R) for n in ("at_o_h", "at_o_l"))
        negmax, rowsum, rinv = (sb(n, [P, NH, NTILE]) for n in ("at_negmax", "at_rowsum", "at_rinv"))
        slots = [ps(f"at_slot{i}", [P, 2, 512]) for i in range(2)]
        banks = [ps(f"at_bank{i}", [P, 512]) for i in range(2)]
        o_ps = ps("at_o", [P, 2, 512])
        stage = prob[:, :, :, :].rearrange("p a t n -> p (a t n)")

        w_in = [sem(f"at_w_in{i}") for i in range(3)]
        ident_ok = sem("at_ident_ok")
        w_hi, w_lo, w_sent = sem("at_w_hi"), sem("at_w_lo"), sem("at_const")
        ln = LayerNorm(sem, "at_ln", h, hn, stats, mv, rstd)
        slot_full = Tally(sem("at_slot_full"), NSLOT)
        bank_full = Tally(sem("at_bank_full"), NBANK)
        o_full = Tally(sem("at_o_full"), NH)
        v_full = Tally(sem("at_v_full"), NTILE)
        tr_h, tr_l = Tally(sem("at_tr_h"), 2), Tally(sem("at_tr_l"), 2)
        v_h, v_l = Tally(sem("at_v_h"), NTILE), Tally(sem("at_v_l"), NTILE)
        proj_h, proj_l = Tally(sem("at_proj_h"), NH), Tally(sem("at_proj_l"), NH)
        stacked = [Tally(sem(f"at_stacked{i}"), NP // 2 * 128) for i in range(2)]
        max_ok = Tally(sem("at_max_ok"), NH * NTILE)
        exp_ok = Tally(sem("at_exp_ok"), NH * NTILE)
        ptr_h, ptr_l = Tally(sem("at_ptr_h"), NH * 6), Tally(sem("at_ptr_l"), NH * 6)
        out_h, out_l = Tally(sem("at_out_h"), NH), Tally(sem("at_out_l"), NH)
        rinv_ok = Tally(sem("at_rinv_ok"), NH)
        added = Tally(sem("at_added"), 2 * NH)
        taken = sem("at_taken")
        pro_full = sem("at_pro_full")
        block = ctx.enter_context(nc.Block())

        def stack_count(p):
            return (p + 1) // 2 * 128

        def pair_before(p):
            return (p - 1) % NP

        def full_wait(eng, it, step):
            if ahead(it):
                eng.wait_ge(pro_full, PRO.index(step) + 1)
            else:
                slot_full.wait(eng, it, slot_of[step] + 1)

        def transposed(dst, k, i):
            bank = banks[k % 2]
            if i == 0:
                return [(dst[:, 0:4, NX:N], bank[:, 0:P].rearrange("p (t n) -> p t n", n=NT)),
                        (dst[0:NT, 4, NX:N], bank[0:NT, P:P + NT])]
            kw = TQ[i - 1]
            return [(dst[0:kw, i - 1, 0:NX], bank[0:kw, :])]

        def slot_view(k, tq, width):
            return slots[k % 2][0:tq, :, 0:width]

        def v_halves(t):
            return [o_ps[:, a, :] for a in range(2)] if t % 2 == 0 else [banks[a][:, :] for a in range(2)]

        def wait_slot_free(eng, b, k):
            for back in range(1, NSLOT + 1):
                if (k - back) % NSLOT % 2 == k % 2:
                    break
            unit = slot_users[(k - back) % NSLOT]
            kind = unit[0]
            tally, count = {
                "TR": lambda: (tr_l, unit[1] + 1),
                "QK": lambda: (proj_l, qk_index[unit] + 1),
                "S": lambda: (exp_ok, unit[1] * NTILE + unit[2] + 1),
                "Y": lambda: (added, 2 * unit[1] + 1),
            }[kind]()
            tally.wait(eng, b, count - (tally.per if k < back else 0))

        def wait_bank_free(eng, b, k):
            prev = (k - 2) % NBANK
            unit = list(bank_of)[prev]
            if unit[0] == "T":
                ptr_l.wait(eng, b, unit[1] * 6 + unit[2] + 1 - (ptr_l.per if k < 2 else 0))
            else:
                added.wait(eng, b, 2 * unit[1] + 2 - (added.per if k < 2 else 0))

        @block.sync
        def _(sp):
            stacked[0].start(sp, 128)
            stacked[1].start(sp)
            sp.dma_start(stage[:, 0:W3], w0_d).then_inc(w_in[0], 16)
            sp.dma_start(stage[:, W3:2 * W3], w1_d).then_inc(w_in[1], 16)
            sp.wait_ge(w_lo, 2)
            sp.dma_start(stage[:, 0:NH * D], wo_d).then_inc(w_in[2], 16)

            def stack(it, p):
                s = stacked[p % 2].sem
                a, z = slice(0, HD), slice(HD, P)
                proj_l.wait(sp, it, qk_index[("QK", p, 0)] + 1)
                for dst, src in ((q_s[a, p % 2, 0], qk_h[a, 0]), (q_s[z, p % 2, 0], q_l[a]),
                                 (q_s[z, p % 2, 1], qk_h[z, 0]), (q_s[a, p % 2, 1], q_l[z])):
                    sp.dma_start(dst.bitcast(F32), src.bitcast(F32)).then_inc(s, 16)
                proj_h.wait(sp, it, qk_index[("QK", p, 1)] + 1)
                for dst, src in ((k_s[a, p % 2, 0], qk_h[a, 1]), (k_s[z, p % 2, 0], qk_h[a, 1]),
                                 (k_s[z, p % 2, 1], qk_h[z, 1]), (k_s[a, p % 2, 1], qk_h[z, 1])):
                    sp.dma_start(dst.bitcast(F32), src.bitcast(F32)).then_inc(s, 16)

            stack(-1, 0)
            with sp.Fori(0, NB) as b:
                for p in [*range(1, NP), 0]:
                    stack(b, p)

        @block.gpsimd
        def _(pool):
            ln.rstd_ok.start(pool, 2)
            pool.memset(ident[:, :], 0.0).then_inc(ident_ok, 1)
            pool.memset(rstd[:, :, :], -0.5).then_inc(ident_ok, 1)
            pool.memset(mv[:, :, :], 1.0).then_inc(ident_ok, 1)
            pool.memset(rowsum[:, :, :], 1.0).then_inc(ident_ok, 1)
            pool.wait_ge(ident_ok, 4)
            pool.affine_select(out=ident[:, :], in_=ident[:, :], compare_op=ALU.not_equal, fill=1.0, base=0,
                               pattern=[[-1, P]], channel_multiplier=1).then_inc(ident_ok, 1)
            ln.scale(pool, -1)
            with pool.Fori(0, NB) as b:
                ln.scale(pool, b)

        @block.scalar
        def _(act):
            for s in (v_h, exp_ok, ptr_h, out_h):
                s.start(act)
            tr_h.start(act, 2)
            proj_h.start(act, 2)
            act.wait_ge(w_in[0], 16)
            act.activation(w0h[:, :], stage[:, 0:W3], ACT.Copy).then_inc(w_hi, 1)
            act.wait_ge(w_in[1], 16)
            act.activation(w1h[:, :], stage[:, W3:2 * W3], ACT.Copy).then_inc(w_hi, 1)
            act.wait_ge(w_in[2], 16)
            act.activation(woh[:, :, :].rearrange("p h d -> p (h d)"), stage[:, 0:NH * D],
                           ACT.Copy).then_inc(w_hi, 1)
            act.wait_ge(ident_ok, 5)
            act.wait_ge(w_lo, 3)

            def run(order, b):
                for step in order:
                    kind = step[0]
                    if kind == "TR":
                        full_wait(act, b, step)
                        src = slots[slot_of[step] % 2][:, :, :].rearrange("p a n -> p (a n)")[:, 0:N]
                        act.activation((x1s if step[1] else x0h)[:, :], src, ACT.Copy).then_inc(tr_h.sem, 1)
                    elif kind == "V":
                        t = step[1]
                        v_full.wait(act, b, t + 1)
                        for a in range(2):
                            src = v_halves(t)[a][0:TQ[t], 0:6 * HD].rearrange("p (h n) -> p h n", n=HD)
                            last = act.activation(v_s[0:TQ[t], t, 6 * a:6 * a + 6, 0:HD], src, ACT.Copy)
                        last.then_inc(v_h.sem, 1)
                    elif kind == "QK":
                        p, m = step[1:]
                        full_wait(act, b, step)
                        if not ahead(b):
                            stacked[pair_before(p) % 2].wait(act, b, stack_count(pair_before(p)))
                        act.activation(qk_h[:, m, :].rearrange("p (a n) -> p a n", a=2), slot_view(slot_of[step], P, HALF),
                                       ACT.Copy, scale=(0.125 if m == 0 else 1.0)).then_inc(proj_h.sem, 1)
                    elif kind == "S":
                        n, i = step[1:]
                        tq = TQ[i]
                        max_ok.wait(act, b, n * NTILE + i + 1)
                        act.activation(prob[0:tq, n % 2, i, :].rearrange("p (a n) -> p a n", a=2),
                                       slot_view(slot_of[step], tq, HALF), ACT.Exp, bias=negmax[0:tq, n, i:i + 1],
                                       accum_out=rowsum[0:tq, n, i:i + 1]).then_inc(exp_ok.sem, 1)
                    elif kind == "T":
                        n, i = step[1:]
                        bank_full.wait(act, b, bank_of[step] + 1)
                        for dst, src in transposed(pt_h, bank_of[step], i):
                            last = act.activation(dst, src, ACT.Copy)
                        last.then_inc(ptr_h.sem, 1)
                    elif kind == "PV" and step[2] == NTILE - 1:
                        o_full.wait(act, b, step[1] + 1)
                        act.activation(o_h[:, :].rearrange("p (a n) -> p a n", a=2), o_ps[:, :, 0:HALF],
                                       ACT.Copy).then_inc(out_h.sem, 1)

            run([s for s in PRO], -1)
            with act.Fori(0, NB) as b:
                run(act_steps, b)

        @block.vector
        def _(dve):
            for s in (v_l, max_ok, ptr_l, out_l, rinv_ok, added):
                s.start(dve)
            ln.start(dve, True)
            tr_l.start(dve, 2)
            proj_l.start(dve, 2)
            dve.wait_ge(w_hi, 1)
            dve.tensor_tensor(w0l[:, :], stage[:, 0:W3], w0h[:, :].bitcast(F32), ALU.subtract).then_inc(w_lo, 1)
            dve.wait_ge(w_hi, 2)
            dve.tensor_tensor(w1l[:, :], stage[0:D1, W3:2 * W3], w1h[0:D1, :].bitcast(F32),
                              ALU.subtract).then_inc(w_lo, 1)
            dve.wait_ge(w_hi, 3)
            dve.tensor_tensor(wol[:, :, :].rearrange("p h d -> p (h d)"), stage[:, 0:NH * D],
                              woh[:, :, :].rearrange("p h d -> p (h d)").bitcast(F32),
                              ALU.subtract).then_inc(w_lo, 1)
            dve.wait_ge(ident_ok, 5)

            def run(order, b):
                for step in order:
                    kind = step[0]
                    if kind in ("LS", "LM", "LA"):
                        following = (b + 1) % NB
                        if kind == "LS":
                            ln.sums(dve, following, step[1])
                        elif kind == "LM":
                            ln.moments(dve, b, step[1])
                        else:
                            ln.apply(dve, b, following, step[1])
                    if kind == "TR":
                        m = step[1]
                        src = slots[slot_of[step] % 2][:, :, :].rearrange("p a n -> p (a n)")
                        tr_h.wait(dve, b, m + 1)
                        if m == 0:
                            dve.tensor_tensor(x0l[:, :], src[:, 0:N], x0h[:, :].bitcast(F32),
                                              ALU.subtract).then_inc(tr_l.sem, 1)
                        else:
                            dve.tensor_tensor(x1s[D1:P, :], src[D1:P, 0:N], x1s[D1:P, :].bitcast(F32),
                                              ALU.subtract).then_inc(tr_l.sem, 1)
                    elif kind == "V":
                        t = step[1]
                        v_h.wait(dve, b, t + 1)
                        for a in range(2):
                            src = v_halves(t)[a][0:TQ[t], 0:6 * HD].rearrange("p (h n) -> p h n", n=HD)
                            hs = slice(6 * a, 6 * a + 6)
                            last = dve.tensor_tensor(v_s[0:TQ[t], t, hs, HD:2 * HD], src,
                                                     v_s[0:TQ[t], t, hs, 0:HD].bitcast(F32), ALU.subtract)
                        last.then_inc(v_l.sem, 1)
                    elif kind == "QK":
                        p, m = step[1:]
                        proj_h.wait(dve, b, qk_index[step] + 1)
                        low = (k_l[:, p % 2, :] if m else q_l[:, :]).rearrange("p (a n) -> p a n", a=2)
                        dve.scalar_tensor_tensor(low, slot_view(slot_of[step], P, HALF), (1.0 if m else 0.125),
                                                 qk_h[:, m, :].rearrange("p (a n) -> p a n", a=2).bitcast(F32),
                                                 ALU.mult, ALU.subtract).then_inc(proj_l.sem, 1)
                    elif kind == "S":
                        n, i = step[1:]
                        tq = TQ[i]
                        full_wait(dve, b, step)
                        dve.tensor_reduce(negmax[0:tq, n, i:i + 1], slot_view(slot_of[step], tq, HALF), AXXY,
                                          ALU.max, negate=True).then_inc(max_ok.sem, 1)
                    elif kind == "T":
                        n, i = step[1:]
                        ptr_h.wait(dve, b, n * 6 + i + 1)
                        for (dst, src), (high, _) in zip(transposed(pt_l, bank_of[step], i),
                                                         transposed(pt_h, bank_of[step], i)):
                            last = dve.tensor_tensor(dst, src, high.bitcast(F32), ALU.subtract)
                        last.then_inc(ptr_l.sem, 1)
                        if i == 0:
                            exp_ok.wait(dve, b, (n + 1) * NTILE)
                            dve.reciprocal(rinv[:, n, :], rowsum[:, n, :]).then_inc(rinv_ok.sem, 1)
                    elif kind == "PV" and step[2] == NTILE - 1:
                        out_h.wait(dve, b, step[1] + 1)
                        dve.tensor_tensor(o_l[:, :].rearrange("p (a n) -> p a n", a=2), o_ps[:, :, 0:HALF],
                                          o_h[:, :].rearrange("p (a n) -> p a n", a=2).bitcast(F32),
                                          ALU.subtract).then_inc(out_l.sem, 1)
                    elif kind == "Y":
                        n = step[1]
                        rinv_ok.wait(dve, b, n + 1)
                        added.wait(dve, b, 2 * n)
                        full_wait(dve, b, step)
                        for t, tq in enumerate(TQ):
                            if t < 4:
                                src = slots[slot_of[step] % 2][0:tq, t // 2, (t % 2) * D:(t % 2 + 1) * D]
                            else:
                                bank_full.wait(dve, b, bank_of[step] + 1)
                                src = banks[bank_of[step] % 2][0:tq, 0:D]
                            row = rows_of(h, b, t)
                            last = dve.scalar_tensor_tensor(row, src, rinv[0:tq, n, t:t + 1], row, ALU.mult, ALU.add)
                            if t >= 3:
                                last.then_inc(added.sem, 1)

            ln.whole(dve, -1, 0)
            run(PRO, -1)
            with dve.Fori(0, NB) as b:
                run(steps, b)

        @block.tensor
        def _(pe):
            for s in (slot_full, bank_full, o_full, v_full):
                s.start(pe)
            pe.wait_ge(w_lo, 3)
            pe.wait_ge(ident_ok, 5)

            def run(order, b):
                for step in order:
                    kind = step[0]
                    done = slot_full.sem if not ahead(b) else pro_full
                    if step in slot_of:
                        slot = slots[slot_of[step] % 2]
                        if not ahead(b):
                            wait_slot_free(pe, b, slot_of[step])
                        elif PRO.index(step) == 1:
                            tr_l.wait(pe, b, 1)
                        elif PRO.index(step) == 3:
                            proj_l.wait(pe, b, qk_index[step])
                    if kind == "TR":
                        m = step[1]
                        ln.hn_ok.wait(pe, b, NTILE)
                        take_wait(pe, taken)
                        flat = slot[:, :, :].rearrange("p a n -> p (a n)")
                        for t, tq in enumerate(TQ):
                            last = pe.transpose(flat[:, t * P:t * P + tq], hn[0:tq, t, m * P:(m + 1) * P],
                                                ident[0:tq, 0:tq])
                        last.then_inc(done, 1)
                    elif kind == "V":
                        t = step[1]
                        if t == 0:
                            tr_l.wait(pe, b, 0)
                            out_l.wait(pe, b, 0)
                        elif t == 1:
                            ptr_l.wait(pe, b, 0)
                            added.wait(pe, b, 0)
                        else:
                            v_l.wait(pe, b, t - 1)
                        rows = slice(t * P, t * P + TQ[t])
                        for a in range(2):
                            cols = slice(2 * NH * HD + a * 6 * HD, 2 * NH * HD + (a + 1) * 6 * HD)
                            terms = [(x0h[:, rows], w0h[:, cols]), (x0l[:, rows], w0h[:, cols]),
                                     (x0h[:, rows], w0l[:, cols]), (x1s[:, rows], w1h[:, cols]),
                                     (x1s[0:D1, rows], w1l[:, cols])]
                            for j, (lhs, rhs) in enumerate(terms):
                                last = pe.matmul(v_halves(t)[a][0:TQ[t], 0:6 * HD], lhs, rhs,
                                                 start=(j == 0), stop=(j == 4))
                        last.then_inc(v_full.sem, 1)
                    elif kind == "QK":
                        p, m = step[1:]
                        if p == 0:
                            tr_l.wait(pe, b, 2)
                        cols = slice(m * NH * HD + p * P, m * NH * HD + (p + 1) * P)
                        for a in range(2):
                            rows = slice(a * HALF, (a + 1) * HALF)
                            terms = [(w0h[:, cols], x0h[:, rows]), (w0h[:, cols], x0l[:, rows]),
                                     (w0l[:, cols], x0h[:, rows]), (w1h[:, cols], x1s[:, rows]),
                                     (w1l[:, cols], x1s[0:D1, rows])]
                            for j, (lhs, rhs) in enumerate(terms):
                                last = pe.matmul(slot[:, a, 0:HALF], lhs, rhs, start=(j == 0), stop=(j == 4))
                        last.then_inc(done, 1)
                    elif kind == "S":
                        n, i = step[1:]
                        tq, par, e = TQ[i], n // 2 % 2, n % 2
                        if i == 0 and e == 0:
                            stacked[par].wait(pe, b, stack_count(n // 2))
                            proj_l.wait(pe, b, n)
                        q = slice(i * P, i * P + tq)
                        own = slice(e * HD, (e + 1) * HD)
                        for a in range(2):
                            k = slice(a * HALF, (a + 1) * HALF)
                            pe.matmul(slot[0:tq, a, 0:HALF], q_s[:, par, e, q], k_s[:, par, e, k], start=True, stop=False)
                            last = pe.matmul(slot[0:tq, a, 0:HALF], q_s[own, par, e, q], k_l[own, par, k],
                                             start=False, stop=True)
                        last.then_inc(done, 1)
                    elif kind == "T":
                        n, i = step[1:]
                        k = bank_of[step]
                        wait_bank_free(pe, b, k)
                        if k == 0:
                            v_l.wait(pe, b, NTILE)
                        exp_ok.wait(pe, b, (n + 1) * NTILE)
                        take_wait(pe, taken)
                        bank = banks[k % 2]
                        if i == 0:
                            for t, kw in enumerate(TQ):
                                last = pe.transpose(bank[0:kw, t * NT:(t + 1) * NT],
                                                    prob[0:NT, n % 2, 4, t * P:t * P + kw], ident[0:NT, 0:NT])
                        else:
                            kw = TQ[i - 1]
                            for t in range(4):
                                last = pe.transpose(bank[0:kw, t * P:(t + 1) * P],
                                                    prob[:, n % 2, t, (i - 1) * P:(i - 1) * P + kw], ident[:, :])
                        last.then_inc(bank_full.sem, 1)
                    elif kind == "PV":
                        n, t = step[1:]
                        ptr_l.wait(pe, b, n * 6 + t + 2)
                        if t == 0:
                            v_l.wait(pe, b, NTILE)
                            out_l.wait(pe, b, n)
                        kw = TQ[t]
                        for a in range(2):
                            q = slice(a * HALF, (a + 1) * HALF)
                            pe.matmul(o_ps[:, a, 0:HALF], v_s[0:kw, t, n, :], pt_h[0:kw, t, q],
                                      start=(t == 0), stop=False)
                            last = pe.matmul(o_ps[:, a, 0:HALF], v_s[0:kw, t, n, :], pt_l[0:kw, t, q],
                                             start=False, stop=(t == NTILE - 1))
                        if t == NTILE - 1:
                            last.then_inc(o_full.sem, 1)
                    elif kind == "Y":
                        n = step[1]
                        out_l.wait(pe, b, n + 1)
                        for t, tq in enumerate(TQ):
                            if t < 4:
                                dst = slot[0:tq, t // 2, (t % 2) * D:(t % 2 + 1) * D]
                            else:
                                wait_bank_free(pe, b, bank_of[step])
                                dst = banks[bank_of[step] % 2][0:tq, 0:D]
                            rows = slice(t * P, t * P + tq)
                            for j, (lhs, rhs) in enumerate(((o_h, woh), (o_l, woh), (o_h, wol))):
                                last = pe.matmul(dst, lhs[:, rows], rhs[:, n, :], start=(j == 0), stop=(j == 2))
                            if t == 3:
                                last.then_inc(done, 1)
                        last.then_inc(bank_full.sem, 1)

            run(PRO, -1)
            with pe.Fori(0, NB) as b:
                run(steps, b)


def ffn_phase(nc, sem, h, aps):
    phi0_d, phi1_d, w1a_d, w1b_d, b1_d, w2_d, b2_d, out_d = aps
    order = [("TR", 0), ("TR", 1)] + [("L", t) for t in range(NTILE)] + [("LT", m) for m in range(NM)]
    order += [("CT", m) for m in range(NM)] + [("DT", t) for t in range(NTILE)] + [("SL", 0), ("SL", 1)]
    order += [("H", 0, 0), ("H", 0, 1)]
    for e in range(1, NE):
        order += [("H", e, 0), ("H", e, 1), ("Y", e - 1)]
    order += [("Y", NE - 1)] + [("O", t) for t in range(NTILE)]
    NU = len(order)
    at = {u: i for i, u in enumerate(order)}
    NSLOTS = 4
    with ExitStack() as ctx:
        def sb(name, shape, dt=F32):
            return ctx.enter_context(nc.sbuf_tensor(name, shape, dt))
        ident = sb("ff_ident", [P, P])
        hn = sb("ff_hn", [P, NTILE, D])
        stats = sb("ff_stats", [P, NTILE, 6])
        mv = sb("ff_mv", [P, NTILE, 2])
        rstd = sb("ff_rstd", [P, 3, NTILE])
        phi0, phi1 = sb("ff_phi0", [P, ES]), sb("ff_phi1", [D1, ES])
        w1a, w1b = sb("ff_w1a", [P, NE, FH]), sb("ff_w1b", [D1, NE, FH])
        b1, b2 = sb("ff_b1", [P, NE * FM]), sb("ff_b2", [P, NE, D])
        w2 = sb("ff_w2", [P, NE, FM, D])
        x0, x1 = sb("ff_x0", [P, N]), sb("ff_x1", [D1, N])
        logit = sb("ff_logit", [P, NTILE, ES])
        comb = sb("ff_comb", [P, NTILE, ES])
        disp = sb("ff_disp", [P, NM, N])
        comb_t = sb("ff_comb_t", [P, NM, N])
        s0, s1 = sb("ff_s0", [P, ES]), sb("ff_s1", [D1, ES])
        hid = sb("ff_hid", [P, 2, FM, NS])
        y = sb("ff_y", [P, NM, D])
        fin = sb("ff_fin", [P, NTILE, D])
        nmc, sumc, rc = (sb(n, [P, NTILE]) for n in ("ff_nmc", "ff_sumc", "ff_rc"))
        nmd, sumd, rd = (sb(n, [P, NM]) for n in ("ff_nmd", "ff_sumd", "ff_rd"))
        slots = [ctx.enter_context(nc.psum_tensor(f"ff_slot{i}", [P, 1024], F32)) for i in range(NSLOTS)]

        w_in = sem("ff_w_in")
        const_ok = sem("ff_const")
        taken = sem("ff_taken")
        ln = LayerNorm(sem, "ff_ln", h, hn, stats, mv, rstd)
        full = Tally(sem("ff_full"), NU)
        tr_out = Tally(sem("ff_tr_out"), 2)
        maxc = Tally(sem("ff_maxc"), NTILE)
        logit_out = Tally(sem("ff_logit_out"), NTILE)
        comb_ok = Tally(sem("ff_comb_ok"), NTILE)
        rc_ok = Tally(sem("ff_rc_ok"), 1)
        maxd = Tally(sem("ff_maxd"), NM)
        disp_exp = Tally(sem("ff_disp_exp"), NM)
        rd_ok = Tally(sem("ff_rd_ok"), NM)
        disp_ok = Tally(sem("ff_disp_ok"), NM)
        ct_out = Tally(sem("ff_ct_out"), NM)
        dt_out = Tally(sem("ff_dt_out"), NTILE)
        sl_out = Tally(sem("ff_sl_out"), 2)
        hid_ok = Tally(sem("ff_hid_ok"), 2 * NE)
        y_ok = Tally(sem("ff_y_ok"), NE)
        fin_ok = Tally(sem("ff_fin_ok"), NTILE)
        sent = Tally(sem("ff_sent"), 32)
        block = ctx.enter_context(nc.Block())

        def normalise(dve, b, m):
            disp_exp.wait(dve, b, m + 1)
            dve.reciprocal(rd[:, m:m + 1], sumd[:, m:m + 1]).then_inc(rd_ok.sem, 1)
            rd_ok.wait(dve, b, m + 1)
            dve.tensor_scalar(disp[:, m, :], disp[:, m, :], rd[:, m:m + 1], None, ALU.mult).then_inc(disp_ok.sem, 1)

        def released(u):
            return {
                "TR": lambda: (tr_out, u[1] + 1),
                "L": lambda: (logit_out, u[1] + 1),
                "LT": lambda: (disp_exp, u[1] + 1),
                "CT": lambda: (ct_out, u[1] + 1),
                "DT": lambda: (dt_out, u[1] + 1),
                "SL": lambda: (sl_out, u[1] + 1),
                "H": lambda: (hid_ok, 2 * u[1] + u[2] + 1),
                "Y": lambda: (y_ok, u[1] + 1),
                "O": lambda: (fin_ok, u[1] + 1),
            }[u[0]]()

        def slot(u):
            return slots[at[u] % NSLOTS]

        def slot_free(eng, b, u):
            k, back = at[u], 1
            while (k - back) % NU % NSLOTS != k % NSLOTS:
                back += 1
            unit = order[(k - back) % NU]
            if (u[0], unit[0]) in (("L", "TR"), ("LT", "L"), ("SL", "DT"), ("H", "SL"), ("Y", "H"), ("O", "Y")):
                return
            tally, count = released(unit)
            tally.wait(eng, b, count - (tally.per if k < back else 0))

        @block.sync
        def _(sp):
            sent.start(sp)
            for dst, src in ((phi0, phi0_d), (phi1, phi1_d), (w1a, w1a_d), (w1b, w1b_d), (b1, b1_d),
                             (b2, b2_d), (w2, w2_d)):
                flat = dst[:]
                if len(dst.shape) == 3:
                    flat = dst[:, :, :].rearrange("p a b -> p (a b)")
                elif len(dst.shape) == 4:
                    flat = dst[:, :, :, :].rearrange("p a b c -> p (a b c)")
                sp.dma_start(flat, src).then_inc(w_in, 16)
            with sp.Fori(0, NB) as b:
                main = out_d[bass.ds(b, 1), 0:NX, :].rearrange("o (t p) d -> p (o t) d", p=P)
                tail = out_d[bass.ds(b, 1), NX:N, :].rearrange("o n d -> (o n) d")
                fin_ok.wait(sp, b, NTILE)
                sp.dma_start(main, fin[:, 0:4, :]).then_inc(sent.sem, 16)
                sp.dma_start(tail, fin[0:NT, 4, :]).then_inc(sent.sem, 16)
            sp.wait_ge(sent.sem, (NB + 1) * 32)

        @block.gpsimd
        def _(pool):
            ln.rstd_ok.start(pool)
            pool.memset(ident[:, :], 0.0).then_inc(const_ok, 1)
            pool.memset(rstd[:, :, :], -0.5).then_inc(const_ok, 1)
            pool.memset(mv[:, :, :], 1.0).then_inc(const_ok, 1)
            pool.memset(sumc[:, :], 1.0).then_inc(const_ok, 1)
            pool.wait_ge(const_ok, 4)
            pool.affine_select(out=ident[:, :], in_=ident[:, :], compare_op=ALU.not_equal, fill=1.0, base=0,
                               pattern=[[-1, P]], channel_multiplier=1).then_inc(const_ok, 1)
            with pool.Fori(0, NB) as b:
                ln.scale(pool, b)

        @block.scalar
        def _(act):
            for s in (comb_ok, disp_exp, dt_out, hid_ok):
                s.start(act)
            act.wait_ge(const_ok, 5)
            act.wait_ge(w_in, 7 * 16)
            with act.Fori(0, NB) as b:
                for u in order:
                    kind = u[0]
                    if kind == "L":
                        t, tq = u[1], TQ[u[1]]
                        logit_out.wait(act, b, t + 1)
                        act.activation(comb[0:tq, t, :], logit[0:tq, t, :], ACT.Exp, bias=nmc[0:tq, t:t + 1],
                                       accum_out=sumc[0:tq, t:t + 1]).then_inc(comb_ok.sem, 1)
                    elif kind == "LT":
                        m = u[1]
                        maxd.wait(act, b, m + 1)
                        act.activation(disp[:, m, :], slot(u)[:, 0:N], ACT.Exp, bias=nmd[:, m:m + 1],
                                       accum_out=sumd[:, m:m + 1]).then_inc(disp_exp.sem, 1)
                    elif kind == "DT":
                        t, tq = u[1], TQ[u[1]]
                        full.wait(act, b, at[u] + 1)
                        act.activation(logit[0:tq, t, :], slot(u)[0:tq, :], ACT.Copy).then_inc(dt_out.sem, 1)
                    elif kind == "H":
                        e, part = u[1:]
                        full.wait(act, b, at[u] + 1)
                        ms = range(4) if part == 0 else range(4, FM)
                        for m in ms:
                            last = act.activation(hid[:, e % 2, m, :], slot(u)[:, (m - ms[0]) * NS:(m - ms[0] + 1) * NS],
                                                  ACT.Gelu_apprx_tanh, bias=b1[:, e * FM + m:e * FM + m + 1])
                        last.then_inc(hid_ok.sem, 1)

        @block.vector
        def _(dve):
            ln.start(dve, False)
            for s in (tr_out, maxc, logit_out, rc_ok, maxd, rd_ok, disp_ok, ct_out,
                      sl_out, y_ok, fin_ok):
                s.start(dve)
            dve.wait_ge(const_ok, 5)
            dve.wait_ge(w_in, 7 * 16)
            with dve.Fori(0, NB) as b:
                ln.whole(dve, b, b)
                for u in order:
                    kind = u[0]
                    if kind == "TR":
                        full.wait(dve, b, at[u] + 1)
                        dst = x1[:, :] if u[1] else x0[:, :]
                        dve.tensor_copy(dst, slot(u)[0:dst.shape[0], 0:N]).then_inc(tr_out.sem, 1)
                    elif kind == "L":
                        t, tq = u[1], TQ[u[1]]
                        full.wait(dve, b, at[u] + 1)
                        dve.tensor_reduce(nmc[0:tq, t:t + 1], slot(u)[0:tq, :], AXX, ALU.max,
                                          negate=True).then_inc(maxc.sem, 1)
                        dve.tensor_copy(logit[0:tq, t, :], slot(u)[0:tq, :]).then_inc(logit_out.sem, 1)
                    elif kind == "LT":
                        m = u[1]
                        full.wait(dve, b, at[u] + 1)
                        dve.tensor_reduce(nmd[:, m:m + 1], slot(u)[:, 0:N], AXX, ALU.max,
                                          negate=True).then_inc(maxd.sem, 1)
                        if m >= 1:
                            normalise(dve, b, m - 1)
                    elif kind == "CT":
                        m = u[1]
                        if m == 0:
                            normalise(dve, b, NM - 1)
                        full.wait(dve, b, at[u] + 1)
                        dve.tensor_copy(comb_t[:, m, :], slot(u)[:, 0:N]).then_inc(ct_out.sem, 1)
                    elif kind == "SL":
                        full.wait(dve, b, at[u] + 1)
                        dst = s1[:, :] if u[1] else s0[:, :]
                        dve.tensor_copy(dst, slot(u)[0:dst.shape[0], :]).then_inc(sl_out.sem, 1)
                    elif kind == "Y":
                        e = u[1]
                        full.wait(dve, b, at[u] + 1)
                        for st in range(2):
                            last = dve.tensor_tensor(y[:, 2 * e + st, :], slot(u)[:, st * D:(st + 1) * D],
                                                     b2[:, e, :], ALU.add)
                        last.then_inc(y_ok.sem, 1)
                    elif kind == "O":
                        t, tq = u[1], TQ[u[1]]
                        if t == 0:
                            comb_ok.wait(dve, b, NTILE)
                            dve.reciprocal(rc[:, :], sumc[:, :]).then_inc(rc_ok.sem, 1)
                            sent.wait(dve, b, 0)
                            rc_ok.wait(dve, b, 1)
                        full.wait(dve, b, at[u] + 1)
                        row = rows_of(h, b, t)
                        dve.scalar_tensor_tensor(fin[0:tq, t, :], slot(u)[0:tq, 0:D], rc[0:tq, t:t + 1], row,
                                                 ALU.mult, ALU.add).then_inc(fin_ok.sem, 1)

        @block.tensor
        def _(pe):
            full.start(pe)
            pe.wait_ge(const_ok, 5)
            pe.wait_ge(w_in, 7 * 16)
            with pe.Fori(0, NB) as b:
                for u in order:
                    kind = u[0]
                    slot_free(pe, b, u)
                    out = slot(u)
                    if kind == "TR":
                        m = u[1]
                        ln.hn_ok.wait(pe, b, NTILE)
                        take_wait(pe, taken)
                        for t, tq in enumerate(TQ):
                            w = P if m == 0 else D1
                            last = pe.transpose(out[0:w, t * P:t * P + tq], hn[0:tq, t, m * P:m * P + w],
                                                ident[0:tq, 0:tq])
                    elif kind == "L":
                        t, tq = u[1], TQ[u[1]]
                        tr_out.wait(pe, b, 2)
                        for a in range(2):
                            cols = slice(a * 512, (a + 1) * 512)
                            pe.matmul(out[0:tq, cols], x0[:, t * P:t * P + tq], phi0[:, cols], start=True, stop=False)
                            last = pe.matmul(out[0:tq, cols], x1[:, t * P:t * P + tq], phi1[:, cols],
                                             start=False, stop=True)
                    elif kind == "LT":
                        logit_out.wait(pe, b, NTILE)
                        take_wait(pe, taken)
                        for t, tq in enumerate(TQ):
                            last = pe.transpose(out[:, t * P:t * P + tq], logit[0:tq, t, u[1] * P:(u[1] + 1) * P],
                                                ident[0:tq, 0:tq])
                    elif kind == "CT":
                        comb_ok.wait(pe, b, NTILE)
                        take_wait(pe, taken)
                        for t, tq in enumerate(TQ):
                            last = pe.transpose(out[:, t * P:t * P + tq], comb[0:tq, t, u[1] * P:(u[1] + 1) * P],
                                                ident[0:tq, 0:tq])
                    elif kind == "DT":
                        t, tq = u[1], TQ[u[1]]
                        disp_ok.wait(pe, b, NM)
                        take_wait(pe, taken)
                        for m in range(NM):
                            last = pe.transpose(out[0:tq, m * P:(m + 1) * P], disp[:, m, t * P:t * P + tq],
                                                ident[:, :])
                    elif kind == "SL":
                        w = D1 if u[1] else P
                        dt_out.wait(pe, b, NTILE)
                        for a in range(2):
                            cols = slice(a * 512, (a + 1) * 512)
                            for t, tq in enumerate(TQ):
                                last = pe.matmul(out[0:w, cols], hn[0:tq, t, u[1] * P:u[1] * P + w],
                                                 logit[0:tq, t, cols], start=(t == 0), stop=(t == NTILE - 1))
                    elif kind == "H":
                        e, part = u[1:]
                        sl_out.wait(pe, b, 2)
                        ms = range(4) if part == 0 else range(4, FM)
                        for m in ms:
                            dst = out[:, (m - ms[0]) * NS:(m - ms[0] + 1) * NS]
                            pe.matmul(dst, w1a[:, e, m * P:(m + 1) * P], s0[:, e * NS:(e + 1) * NS],
                                      start=True, stop=False)
                            last = pe.matmul(dst, w1b[:, e, m * P:(m + 1) * P], s1[:, e * NS:(e + 1) * NS],
                                             start=False, stop=True)
                    elif kind == "Y":
                        e = u[1]
                        hid_ok.wait(pe, b, 2 * e + 2)
                        for st in range(2):
                            for m in range(FM):
                                last = pe.matmul(out[:, st * D:(st + 1) * D], hid[:, e % 2, m, st * P:(st + 1) * P],
                                                 w2[:, e, m, :], start=(m == 0), stop=(m == FM - 1))
                    elif kind == "O":
                        t, tq = u[1], TQ[u[1]]
                        ct_out.wait(pe, b, NM)
                        y_ok.wait(pe, b, NE)
                        for m in range(NM):
                            last = pe.matmul(out[0:tq, 0:D], comb_t[:, m, t * P:t * P + tq], y[:, m, :],
                                             start=(m == 0), stop=(m == NM - 1))
                    last.then_inc(full.sem, 1)


def early_fusion_kernel(nc, x_d, txt_d, f_d, wtok_d, w0_d, w1_d, wo_d,
                        phi0_d, phi1_d, w1a_d, w1b_d, b1_d, w2_d, b2_d, out_d):
    with ExitStack() as ctx:
        def sem(name):
            return ctx.enter_context(nc.semaphore(name))
        h = ctx.enter_context(nc.sbuf_tensor("h", [P, NB * NTILE, D], F32))
        tok_phase(nc, sem, h, (x_d, wtok_d, f_d, txt_d))
        attn_phase(nc, sem, h, (w0_d, w1_d, wo_d))
        ffn_phase(nc, sem, h, (phi0_d, phi1_d, w1a_d, w1b_d, b1_d, w2_d, b2_d, out_d))


def laid_out(x, txt, freq, w_tok, w_qkv, w_o, phi, w1, b1, w2, b2):
    import numpy as np
    c = np.ascontiguousarray
    xt = x.reshape(NB, NX, 3 * D).transpose(0, 2, 1)
    full = (CH - 1) * P
    x_l = np.concatenate([xt[:, :full].reshape(NB, CH - 1, P, NX),
                          np.concatenate([xt[:, full:], xt[:, full:]], 1)[:, None]], 1)
    wt = w_tok.reshape(D, 3 * D, 2, BANDS).transpose(2, 3, 1, 0)
    units = [wt[kind, 2 * jp + jj, ch * P:(ch + 1) * P]
             for ch in range(CH - 1) for jp in range(3) for kind in range(2) for jj in range(2)]
    units += [np.concatenate([wt[0, j, full:], wt[1, j, full:]]) for j in range(BANDS)]
    qkv = w_qkv.transpose(2, 1, 0, 3).reshape(D, 3 * NH * HD)
    wo = w_o.reshape(NH, HD, D).transpose(1, 0, 2).reshape(HD, NH * D)
    phi_t = phi.reshape(ES, D).T
    w1_t = w1.transpose(1, 0, 2).reshape(D, NE * FH)
    return {
        "x": c(x_l), "txt": c(txt), "freq": c(np.broadcast_to(freq, (P, BANDS))),
        "w_tok": c(np.stack(units, 1).reshape(P, NKU * D)),
        "w_qkv0": c(qkv[:P]), "w_qkv1": c(np.concatenate([qkv[P:], qkv[P:]])), "w_o": c(np.concatenate([wo, wo])),
        "phi0": c(phi_t[:P]), "phi1": c(phi_t[P:]), "w1a": c(w1_t[:P]), "w1b": c(w1_t[P:]),
        "b1": c(b1.reshape(NE * FM, P).T),
        "w2": c(w2.reshape(NE, FM, P, D).transpose(2, 0, 1, 3).reshape(P, NE * FM * D)),
        "b2": c(np.broadcast_to(b2.reshape(1, NE * D), (P, NE * D))),
    }


def kernel(x, txt, L0_tok_freq_bands, L0_tok_W, L0_attn_w_qkv, L0_attn_w_o, L0_ffn_phi, L0_ffn_w1,
           L0_ffn_b1, L0_ffn_w2, L0_ffn_b2):
    import numpy as np
    import concourse.bacc as bacc
    from concourse.bass_utils import run_bass_kernel_spmd

    given = [np.asarray(a) for a in (x, txt, L0_tok_freq_bands, L0_tok_W, L0_attn_w_qkv, L0_attn_w_o, L0_ffn_phi,
                                     L0_ffn_w1, L0_ffn_b1, L0_ffn_w2, L0_ffn_b2)]
    nc = bacc.Bacc("TRN2", target_bir_lowering=False, num_devices=1)
    arrays, args = {}, []
    for name, a in laid_out(*given).items():
        arrays[f"in_{name}_dram"] = a
        args.append(nc.dram_tensor(f"in_{name}_dram", a.shape, mybir.dt.from_np(a.dtype), kind="ExternalInput").ap())
    args.append(nc.dram_tensor("out_0_dram", (NB, N, D), F32, kind="ExternalOutput").ap())
    early_fusion_kernel(nc, *args)
    r = run_bass_kernel_spmd(nc, [arrays], core_ids=[0])
    return r.results[0]["out_0_dram"]
```

```python
from contextlib import ExitStack

import concourse.bass as bass
from concourse import mybir

F32 = mybir.dt.float32
F32R = mybir.dt.float32r
ACT = mybir.ActivationFunctionType
ALU = mybir.AluOpType
AXX = mybir.AxisListType.X
AXXY = mybir.AxisListType.XY

P = 128
NB, NX, NT, D = 8, 512, 32, 192
N = NX + NT
TQ = [128, 128, 128, 128, 32]
NTILE = len(TQ)
HALF = N // 2
D1 = D - P
BANDS = 6
CH = 5
NKU = (CH - 1) * 2 * BANDS + BANDS
EPS = 1e-5
MAGIC = 12582912.0
TWO_PI = 6.2831845
HALF_PI = 1.5707963

NH, HD = 12, 64
NP = NH // 2
NE, NS, FH = 4, 256, 768
ES = NE * NS
NM = ES // P
FM = FH // P


class Tally:

    def __init__(self, sem, per):
        self.sem, self.per = sem, per

    def start(self, eng, ahead=0):
        if self.per > ahead:
            eng.sem_inc(self.sem, self.per - ahead)

    def wait(self, eng, it, k):
        eng.wait_ge(self.sem, it * self.per + (self.per + k))


def tok_phase(nc, sem, h, aps):
    x_d, w_d, f_d, txt_d = aps
    NU = CH * 3
    SLOTS = 3
    made = [0]
    for u in range(NU):
        made.append(made[-1] + (2 if u // 3 < CH - 1 else 1))
    with ExitStack() as ctx:
        def sb(name, shape, dt=F32):
            return ctx.enter_context(nc.sbuf_tensor(name, shape, dt))
        w = sb("tok_w", [P, NKU, D])
        freq = sb("tok_freq", [P, BANDS])
        x = sb("tok_x", [P, CH, NX])
        shifted = sb("tok_shifted", [P, 2, NX])
        whole = sb("tok_whole", [P, 2, NX])
        turn = sb("tok_turn", [P, SLOTS, 2, NX])
        absturn = sb("tok_absturn", [P, SLOTS, 2, NX])
        feat = sb("tok_feat", [P, SLOTS, 2, 2, NX])
        sc = sb("tok_sc", [P, 3])
        acc = [ctx.enter_context(nc.psum_tensor(f"tok_acc{t}", [P, 512], F32)) for t in range(4)]

        w_in = [sem(f"tok_w_in{c}") for c in range(CH)]
        f_in = sem("tok_f_in")
        txt_in = sem("tok_txt_in")
        const_ok = sem("tok_const_ok")
        x_in = [Tally(sem(f"tok_x_in{c}"), 16) for c in range(CH)]
        x_used = Tally(sem("tok_x_used"), CH)
        shifted_ok = Tally(sem("tok_shifted_ok"), 2 * NU)
        whole_ok = Tally(sem("tok_whole_ok"), NU)
        turn_ok = Tally(sem("tok_turn_ok"), 2 * NU)
        abs_ok = Tally(sem("tok_abs_ok"), NU)
        feat_ok = Tally(sem("tok_feat_ok"), made[-1])
        feat_used = Tally(sem("tok_feat_used"), NU)
        acc_ok = Tally(sem("tok_acc_ok"), 3)
        acc_out = Tally(sem("tok_acc_out"), 4)
        block = ctx.enter_context(nc.Block())

        @block.sync
        def _(sp):
            for c in range(CH):
                x_in[c].start(sp)
            sp.dma_start(freq[:, :], f_d).then_inc(f_in, 16)
            for c in range(CH):
                sp.dma_start(x[:, c, :], x_d[0, c]).then_inc(x_in[c].sem, 16)
                k0, k1 = 2 * BANDS * c, min(2 * BANDS * (c + 1), NKU)
                sp.dma_start(w[:, k0:k1, :].rearrange("p k n -> p (k n)"), w_d[:, k0 * D:k1 * D]).then_inc(w_in[c], 16)
            sp.dma_start(h[0:NT, NTILE - 1:NB * NTILE:NTILE, :],
                         txt_d.rearrange("b n d -> n b d")).then_inc(txt_in, 16)
            with sp.Fori(0, NB - 1) as b:
                for c in range(CH):
                    src = x_d[bass.ds(b + 1, 1), c].rearrange("o p n -> (o p) n")
                    x_used.wait(sp, b, c + 1)
                    sp.dma_start(x[:, c, :], src).then_inc(x_in[c].sem, 16)
            sp.wait_ge(txt_in, 16)

        @block.vector
        def _(dve):
            for s in (x_used, shifted_ok, whole_ok, turn_ok, abs_ok):
                s.start(dve)
            dve.memset(sc[0:D1, 0:1], TWO_PI)
            dve.memset(sc[D1:P, 0:1], -TWO_PI)
            dve.memset(sc[0:D1, 1:2], 0.0)
            dve.memset(sc[D1:P, 1:2], HALF_PI)
            dve.memset(sc[:, 2:3], HALF_PI).then_inc(const_ok, 1)
            dve.wait_ge(f_in, 16)
            with dve.Fori(0, NB) as b:
                for u in range(NU):
                    c, jp, s = u // 3, u % 3, u % SLOTS
                    if jp == 0:
                        x_in[c].wait(dve, b, 16)
                    turn_ok.wait(dve, b, 2 * u)
                    for jj in range(2):
                        j = 2 * jp + jj
                        dve.tensor_scalar(shifted[:, jj, :], x[:, c, :], freq[:, j:j + 1], MAGIC,
                                          ALU.mult, ALU.add).then_inc(shifted_ok.sem, 1)
                    shifted_ok.wait(dve, b, 2 * u + 2)
                    dve.tensor_scalar(whole[:, :, :], shifted[:, :, :], MAGIC, None,
                                      ALU.subtract).then_inc(whole_ok.sem, 1)
                    whole_ok.wait(dve, b, u + 1)
                    prev = u - SLOTS
                    feat_ok.wait(dve, b, made[prev + 1] if prev >= 0 else made[prev + NU + 1] - made[-1])
                    for jj in range(2):
                        j = 2 * jp + jj
                        dve.scalar_tensor_tensor(turn[:, s, jj, :], x[:, c, :], freq[:, j:j + 1],
                                                 whole[:, jj, :], ALU.mult,
                                                 ALU.subtract).then_inc(turn_ok.sem, 1)
                    turn_ok.wait(dve, b, 2 * u + 2)
                    if c < CH - 1:
                        dve.scalar_tensor_tensor(absturn[:, s, :, :], turn[:, s, :, :], -1.0, turn[:, s, :, :],
                                                 ALU.mult, ALU.max).then_inc(abs_ok.sem, 1)
                    else:
                        dve.scalar_tensor_tensor(turn[D1:P, s, :, :], turn[D1:P, s, :, :], -1.0,
                                                 turn[D1:P, s, :, :], ALU.mult,
                                                 ALU.max).then_inc(abs_ok.sem, 1)
                    if jp == 2:
                        dve.sem_inc(x_used.sem, 1)

        @block.scalar
        def _(act):
            feat_ok.start(act)
            acc_out.start(act)
            act.wait_ge(const_ok, 1)

            def units(b, some):
                for u in some:
                    c, s = u // 3, u % SLOTS
                    feat_used.wait(act, b, u - SLOTS + 1)
                    if c < CH - 1:
                        turn_ok.wait(act, b, 2 * u + 2)
                        act.activation(feat[:, s, 0, :, :], turn[:, s, :, :], ACT.Sin,
                                       scale=TWO_PI).then_inc(feat_ok.sem, 1)
                        abs_ok.wait(act, b, u + 1)
                        act.activation(feat[:, s, 1, :, :], absturn[:, s, :, :], ACT.Sin, bias=sc[:, 2:3],
                                       scale=-TWO_PI).then_inc(feat_ok.sem, 1)
                    else:
                        abs_ok.wait(act, b, u + 1)
                        act.activation(feat[:, s, 0, :, :], turn[:, s, :, :], ACT.Sin, bias=sc[:, 1:2],
                                       scale=sc[:, 0:1]).then_inc(feat_ok.sem, 1)

            def copy_out(b):
                for t in range(4):
                    if t < 3:
                        acc_ok.wait(act, b, t + 1)
                    else:
                        feat_used.wait(act, b, NU)
                    act.activation(h[:, bass.ds(b * NTILE + t, 1), :].rearrange("p o d -> p (o d)"),
                                   acc[t][:, 0:D], ACT.Copy).then_inc(acc_out.sem, 1)

            units(0, range(2))
            with act.Fori(0, NB - 1) as b:
                units(b, range(2, NU))
                units(b + 1, range(2))
                copy_out(b)
            units(NB - 1, range(2, NU))
            copy_out(NB - 1)

        @block.tensor
        def _(pe):
            feat_used.start(pe)
            acc_ok.start(pe)
            with pe.Fori(0, NB) as b:
                k = 0
                for u in range(NU):
                    c, s = u // 3, u % SLOTS
                    if u % 3 == 0:
                        pe.wait_ge(w_in[c], 16)
                    for kind in range(2 if c < CH - 1 else 1):
                        feat_ok.wait(pe, b, made[u] + kind + 1)
                        for jj in range(2):
                            for t in range(4):
                                if k == 0:
                                    acc_out.wait(pe, b, t - 3)
                                last = pe.matmul(acc[t][:, 0:D], feat[:, s, kind, jj, t * P:(t + 1) * P],
                                                 w[:, k, :], start=(k == 0), stop=(k == NKU - 1))
                                if k == NKU - 1 and t < 3:
                                    last.then_inc(acc_ok.sem, 1)
                            k += 1
                    last.then_inc(feat_used.sem, 1)



def rows_of(h, batch, t, c0=0, c1=D):
    rows = h[0:TQ[t], bass.ds(batch * NTILE + t, 1), c0:c1]
    return rows.rearrange("p o d -> p (o d)")


class LayerNorm:

    def __init__(self, sem, name, h, hn, stats, mv, rstd):
        self.h, self.hn, self.stats, self.mv, self.rstd = h, hn, stats, mv, rstd
        self.pieces = [(0, D, 0)] + ([(P, D, D)] if hn.shape[2] > D else [])
        self.stats_ok = Tally(sem(name + "_stats"), NTILE)
        self.mv_ok = Tally(sem(name + "_mv"), NTILE)
        self.rstd_ok = Tally(sem(name + "_rstd"), 2)
        self.hn_ok = Tally(sem(name + "_hn"), NTILE)
        self.taken = sem(name + "_taken")

    def start(self, dve, ahead):
        for s in (self.stats_ok, self.mv_ok, self.hn_ok):
            s.start(dve, s.per if ahead else 0)

    def sums(self, dve, batch, t):
        dve.bn_stats(self.stats[0:TQ[t], t, :], rows_of(self.h, batch, t)).then_inc(self.stats_ok.sem, 1)

    def moments(self, dve, it, t):
        self.stats_ok.wait(dve, it, t + 1)
        take_wait(dve, self.taken)
        dve.bn_aggr(self.mv[0:TQ[t], t, :], self.stats[0:TQ[t], t, :]).then_inc(self.mv_ok.sem, 1)

    def scale(self, pool, it):
        self.mv_ok.wait(pool, it, NTILE)
        take_wait(pool, self.taken)
        pool.tensor_scalar(self.rstd[:, 0, :], self.mv[:, :, 1], EPS, None, ALU.add).then_inc(self.rstd_ok.sem, 1)
        self.rstd_ok.wait(pool, it, 1)
        pool.tensor_tensor(self.rstd[:, 1, :], self.rstd[:, 0, :], self.rstd[:, 2, :],
                           ALU.pow).then_inc(self.rstd_ok.sem, 1)

    def apply(self, dve, it, batch, t):
        self.rstd_ok.wait(dve, it, 2)
        for c0, c1, o in self.pieces:
            last = dve.tensor_scalar(self.hn[0:TQ[t], t, o:o + c1 - c0], rows_of(self.h, batch, t, c0, c1),
                                     self.mv[0:TQ[t], t, 0:1], self.rstd[0:TQ[t], 1, t:t + 1],
                                     ALU.subtract, ALU.mult)
        last.then_inc(self.hn_ok.sem, 1)

    def whole(self, dve, it, batch):
        for t in range(NTILE):
            self.sums(dve, batch, t)
        for t in range(NTILE):
            self.moments(dve, it, t)
        for t in range(NTILE):
            self.apply(dve, it, batch, t)


def ahead(it):
    return isinstance(it, int)


def take_wait(eng, taken):
    eng.sem_inc(taken, 1)


ATTN_STAGES = {
    "tensor": ("S0 p2 p3 E0 p4 S1 T0 T1 S2 T2 E1 Q T3 E2 S3 P0 T4 Y E3 S4 T5 E4 P1",
               "S0 E0 p2 p3 Q p4 E1 T0 S1 T1 S2 T2 E2 S3 T3 P0 T4 Y S4 T5 E3 E4 P1"),
    "scalar": ("S0 p4 T0 T1 E0 S1 T2 E1 S2 Q T3 E2 S3 T4 Y E3 E4 T5 S4",
               "S0 Q E0 E1 T0 p4 T1 S1 T2 S2 E2 T3 T4 S3 Y T5 S4 E3 E4"),
    "vector": ("S0 S1 E0 T0 S2 T1 T2 E1 Q S3 E2 T3 T4 Y E3 S4 E4 T5",
               "S0 E0 Q S1 T0 T1 E1 S2 T2 S3 E2 T3 T4 Y S4 T5 E3 E4"),
}


def attn_order(engine):
    steps = []
    for n in range(NH + 2):
        for token in ATTN_STAGES[engine][n % 2].split():
            name, i = token[0], int(token[1:] or 0)
            head = n - {"T": 1, "P": 1, "p": 2, "Y": 2}.get(name, 0)
            if name == "E":
                steps += extra_steps(n, i)
            elif name == "Q":
                if n // 2 + 1 < NP:
                    steps.append(("QK", n // 2 + 1, n % 2))
            elif 0 <= head < NH:
                steps.append(("Y", head) if name == "Y" else ("PV" if name in "pP" else name, head, i))
    return steps


def extra_steps(n, i):
    if n == 0:
        return [("V", i)]
    if n in (6, 7, 8):
        return [(("LS", "LM", "LA")[n - 6], i)]
    if n == 10 and i in (2, 3):
        return [("TR", i - 2)]
    if n == 11 and i in (2, 3):
        return [("QK", 0, i - 2)]
    return []


def attn_phase(nc, sem, h, aps):
    w0_d, w1_d, wo_d = aps
    W3 = 3 * NH * HD
    steps, act_steps, dve_steps = (attn_order(engine) for engine in ("tensor", "scalar", "vector"))
    slot_of = {s: i for i, s in enumerate(x for x in steps if x[0] in ("TR", "QK", "S", "Y"))}
    bank_of = {s: i for i, s in enumerate(x for x in steps if x[0] in ("T", "Y"))}
    slot_users = list(slot_of)
    PRO = [("TR", 0), ("TR", 1), ("QK", 0, 0), ("QK", 0, 1)]
    qk_index = {s: i for i, s in enumerate(x for x in steps if x[0] == "QK")}
    NSLOT, NBANK = len(slot_of), len(bank_of)
    with ExitStack() as ctx:
        def sb(name, shape, dt=F32):
            return ctx.enter_context(nc.sbuf_tensor(name, shape, dt))

        def ps(name, shape):
            return ctx.enter_context(nc.psum_tensor(name, shape, F32))
        ident = sb("at_ident", [P, P])
        hn = sb("at_hn", [P, NTILE, 2 * P])
        stats = sb("at_stats", [P, NTILE, 6])
        mv = sb("at_mv", [P, NTILE, 2])
        rstd = sb("at_rstd", [P, 3, NTILE])
        x0h, x0l, x1s = (sb(n, [P, N], F32R) for n in ("at_x0h", "at_x0l", "at_x1s"))
        w0h, w0l, w1h = (sb(n, [P, W3], F32R) for n in ("at_w0h", "at_w0l", "at_w1h"))
        w1l = sb("at_w1l", [D1, W3], F32R)
        wo = sb("at_wo", [P, NH, D])
        qk_h = sb("at_qk_h", [P, 2, N], F32R)
        q_l = sb("at_q_l", [P, N], F32R)
        k_l = sb("at_k_l", [P, 2, N], F32R)
        q_s = sb("at_q_s", [P, 2, 2, N], F32R)
        k_s = sb("at_k_s", [P, 2, 2, N], F32R)
        v_s = sb("at_v_s", [P, NTILE, NH, 2 * HD], F32R)
        prob = sb("at_prob", [P, 2, NTILE, N])
        pt_h, pt_l = (sb(n, [P, NTILE, N], F32R) for n in ("at_pt_h", "at_pt_l"))
        o_s = sb("at_o_s", [P, N])
        negmax, rowsum, rinv = (sb(n, [P, NH, NTILE]) for n in ("at_negmax", "at_rowsum", "at_rinv"))
        scaled = sb("at_scaled", [P, 2, NTILE - 2, D])
        slots = [ps(f"at_slot{i}", [P, 2, 512]) for i in range(2)]
        banks = [ps(f"at_bank{i}", [P, 512]) for i in range(2)]
        o_ps = ps("at_o", [P, 2, 512])
        stage = prob[:, :, :, :].rearrange("p a t n -> p (a t n)")

        w_in = [sem(f"at_w_in{i}") for i in range(3)]
        ident_ok = sem("at_ident_ok")
        w_hi, w_lo = sem("at_w_hi"), sem("at_w_lo")
        ln = LayerNorm(sem, "at_ln", h, hn, stats, mv, rstd)
        slot_full = Tally(sem("at_slot_full"), NSLOT)
        bank_full = Tally(sem("at_bank_full"), NBANK)
        o_full = Tally(sem("at_o_full"), NH)
        v_full = Tally(sem("at_v_full"), NTILE)
        tr_h, tr_l = Tally(sem("at_tr_h"), 2), Tally(sem("at_tr_l"), 2)
        v_h, v_l = Tally(sem("at_v_h"), NTILE), Tally(sem("at_v_l"), NTILE)
        proj_h, proj_l = Tally(sem("at_proj_h"), NH), Tally(sem("at_proj_l"), NH)
        stacked = [Tally(sem(f"at_stacked{i}"), NP // 2 * 128) for i in range(2)]
        max_ok = Tally(sem("at_max_ok"), NH * NTILE)
        exp_ok = Tally(sem("at_exp_ok"), NH * NTILE)
        ptr_h, ptr_l = Tally(sem("at_ptr_h"), NH * 6), Tally(sem("at_ptr_l"), NH * 6)
        o_out = Tally(sem("at_o_out"), NH)
        rinv_ok = Tally(sem("at_rinv_ok"), NH)
        added, scaled_ok, pool_added = Tally(sem("at_added"), NH), Tally(sem("at_scaled_ok"), 2 * NH), Tally(
            sem("at_pool_added"), 3 * NH)
        taken = sem("at_taken")
        pro_full = sem("at_pro_full")
        block = ctx.enter_context(nc.Block())

        def stack_count(p):
            return (p + 1) // 2 * 128

        def pair_before(p):
            return (p - 1) % NP

        def full_wait(eng, it, step):
            if ahead(it):
                eng.wait_ge(pro_full, PRO.index(step) + 1)
            else:
                slot_full.wait(eng, it, slot_of[step] + 1)

        def transposed(dst, k, i):
            bank = banks[k % 2]
            if i == 0:
                return [(dst[:, 0:4, NX:N], bank[:, 0:P].rearrange("p (t n) -> p t n", n=NT)),
                        (dst[0:NT, 4, NX:N], bank[0:NT, P:P + NT])]
            kw = TQ[i - 1]
            return [(dst[0:kw, i - 1, 0:NX], bank[0:kw, :])]

        def slot_view(k, tq, width):
            return slots[k % 2][0:tq, :, 0:width]

        def v_halves(t):
            return [o_ps[:, a, :] for a in range(2)] if t % 2 == 0 else [banks[a][:, :] for a in range(2)]

        def wait_slot_free(eng, b, k):
            for back in range(1, NSLOT + 1):
                if (k - back) % NSLOT % 2 == k % 2:
                    break
            unit = slot_users[(k - back) % NSLOT]
            kind = unit[0]
            tally, count = {
                "TR": lambda: (tr_l, unit[1] + 1),
                "QK": lambda: (proj_l, qk_index[unit] + 1),
                "S": lambda: (exp_ok, unit[1] * NTILE + unit[2] + 1),
                "Y": lambda: (added, unit[1] + 1),
            }[kind]()
            if kind == "Y":
                scaled_ok.wait(eng, b, 2 * unit[1] + 1 - (scaled_ok.per if k < back else 0))
            tally.wait(eng, b, count - (tally.per if k < back else 0))

        def wait_bank_free(eng, b, k):
            prev = (k - 2) % NBANK
            unit = list(bank_of)[prev]
            if unit[0] == "T":
                ptr_l.wait(eng, b, unit[1] * 6 + unit[2] + 1 - (ptr_l.per if k < 2 else 0))
            else:
                scaled_ok.wait(eng, b, 2 * unit[1] + 2 - (scaled_ok.per if k < 2 else 0))

        @block.sync
        def _(sp):
            stacked[0].start(sp, 128)
            stacked[1].start(sp)
            sp.dma_start(stage[:, 0:W3], w0_d).then_inc(w_in[0], 16)
            sp.dma_start(stage[:, W3:2 * W3], w1_d).then_inc(w_in[1], 16)
            sp.dma_start(wo[:, :, :].rearrange("p h d -> p (h d)"), wo_d).then_inc(w_in[2], 16)

            def stack(it, p):
                s = stacked[p % 2].sem
                a, z = slice(0, HD), slice(HD, P)
                proj_l.wait(sp, it, qk_index[("QK", p, 0)] + 1)
                for dst, src in ((q_s[a, p % 2, 0], qk_h[a, 0]), (q_s[z, p % 2, 0], q_l[a]),
                                 (q_s[z, p % 2, 1], qk_h[z, 0]), (q_s[a, p % 2, 1], q_l[z])):
                    sp.dma_start(dst.bitcast(F32), src.bitcast(F32)).then_inc(s, 16)
                proj_h.wait(sp, it, qk_index[("QK", p, 1)] + 1)
                for dst, src in ((k_s[a, p % 2, 0], qk_h[a, 1]), (k_s[z, p % 2, 0], qk_h[a, 1]),
                                 (k_s[z, p % 2, 1], qk_h[z, 1]), (k_s[a, p % 2, 1], qk_h[z, 1])):
                    sp.dma_start(dst.bitcast(F32), src.bitcast(F32)).then_inc(s, 16)

            stack(-1, 0)
            with sp.Fori(0, NB) as b:
                for p in [*range(1, NP), 0]:
                    stack(b, p)
            sp.wait_ge(stacked[0].sem, (NB + 1) * stacked[0].per)

        @block.gpsimd
        def _(pool):
            ln.rstd_ok.start(pool, 2)
            pool.memset(ident[:, :], 0.0).then_inc(ident_ok, 1)
            pool.memset(rstd[:, :, :], -0.5).then_inc(ident_ok, 1)
            pool.memset(mv[:, :, :], 1.0).then_inc(ident_ok, 1)
            pool.memset(rowsum[:, :, :], 1.0).then_inc(ident_ok, 1)
            pool.wait_ge(ident_ok, 4)
            pool.affine_select(out=ident[:, :], in_=ident[:, :], compare_op=ALU.not_equal, fill=1.0, base=0,
                               pattern=[[-1, P]], channel_multiplier=1).then_inc(ident_ok, 1)
            ln.scale(pool, -1)
            pool_added.start(pool)
            with pool.Fori(0, NB) as b:
                for n in range(NH):
                    if n == 6:
                        ln.scale(pool, b)
                    for t in range(2, NTILE):
                        pool_added.wait(pool, b, 3 * (n - 1) + t - 1)
                        if t != 3:
                            scaled_ok.wait(pool, b, 2 * n + 1 + t // 4)
                        take_wait(pool, ln.taken)
                        row = rows_of(h, b, t)
                        pool.tensor_tensor(row, scaled[0:TQ[t], n % 2, t - 2, :], row,
                                           ALU.add).then_inc(pool_added.sem, 1)

        @block.scalar
        def _(act):
            for s in (v_h, exp_ok, ptr_h, o_out, scaled_ok):
                s.start(act)
            tr_h.start(act, 2)
            proj_h.start(act, 2)
            act.wait_ge(ident_ok, 5)

            def run(order, b):
                for step in order:
                    kind = step[0]
                    if kind == "TR":
                        full_wait(act, b, step)
                        src = slots[slot_of[step] % 2][:, :, :].rearrange("p a n -> p (a n)")[:, 0:N]
                        act.activation((x1s if step[1] else x0h)[:, :], src, ACT.Copy).then_inc(tr_h.sem, 1)
                    elif kind == "V":
                        t = step[1]
                        v_full.wait(act, b, t + 1)
                        for a in range(2):
                            src = v_halves(t)[a][0:TQ[t], 0:6 * HD].rearrange("p (h n) -> p h n", n=HD)
                            last = act.activation(v_s[0:TQ[t], t, 6 * a:6 * a + 6, 0:HD], src, ACT.Copy)
                        last.then_inc(v_h.sem, 1)
                    elif kind == "QK":
                        p, m = step[1:]
                        full_wait(act, b, step)
                        if not ahead(b):
                            stacked[pair_before(p) % 2].wait(act, b, stack_count(pair_before(p)))
                        act.activation(qk_h[:, m, :].rearrange("p (a n) -> p a n", a=2), slot_view(slot_of[step], P, HALF),
                                       ACT.Copy, scale=(0.125 if m == 0 else 1.0)).then_inc(proj_h.sem, 1)
                    elif kind == "S":
                        n, i = step[1:]
                        tq = TQ[i]
                        max_ok.wait(act, b, n * NTILE + i + 1)
                        act.activation(prob[0:tq, n % 2, i, :].rearrange("p (a n) -> p a n", a=2),
                                       slot_view(slot_of[step], tq, HALF), ACT.Exp, bias=negmax[0:tq, n, i:i + 1],
                                       accum_out=rowsum[0:tq, n, i:i + 1]).then_inc(exp_ok.sem, 1)
                    elif kind == "T":
                        n, i = step[1:]
                        bank_full.wait(act, b, bank_of[step] + 1)
                        for dst, src in transposed(pt_h, bank_of[step], i):
                            last = act.activation(dst, src, ACT.Copy)
                        last.then_inc(ptr_h.sem, 1)
                    elif kind == "PV" and step[2] == NTILE - 1:
                        o_full.wait(act, b, step[1] + 1)
                        act.activation(o_s[:, :].rearrange("p (a n) -> p a n", a=2), o_ps[:, :, 0:HALF],
                                       ACT.Copy).then_inc(o_out.sem, 1)
                    elif kind == "Y":
                        n = step[1]
                        rinv_ok.wait(act, b, n + 1)
                        pool_added.wait(act, b, 3 * (n - 1))
                        for t in range(2, NTILE):
                            if t == 2:
                                full_wait(act, b, step)
                                src = slots[slot_of[step] % 2][0:TQ[t], 1, 0:D]
                            elif t == 3:
                                src = slots[slot_of[step] % 2][0:TQ[t], 1, D:2 * D]
                            else:
                                bank_full.wait(act, b, bank_of[step] + 1)
                                src = banks[bank_of[step] % 2][0:TQ[t], 0:D]
                            last = act.activation(scaled[0:TQ[t], n % 2, t - 2, :], src, ACT.Copy,
                                                  scale=rinv[0:TQ[t], n, t:t + 1])
                            if t >= 3:
                                last.then_inc(scaled_ok.sem, 1)

            run(PRO[:2], -1)
            act.wait_ge(w_in[0], 16)
            act.activation(w0h[:, :], stage[:, 0:W3], ACT.Copy).then_inc(w_hi, 1)
            act.wait_ge(w_in[1], 16)
            act.activation(w1h[:, :], stage[:, W3:2 * W3], ACT.Copy).then_inc(w_hi, 1)
            run(PRO[2:], -1)
            act.wait_ge(w_lo, 2)
            with act.Fori(0, NB) as b:
                run(act_steps, b)

        @block.vector
        def _(dve):
            for s in (v_l, max_ok, ptr_l, rinv_ok, added):
                s.start(dve)
            ln.start(dve, True)
            tr_l.start(dve, 2)
            proj_l.start(dve, 2)
            dve.wait_ge(ident_ok, 5)

            def run(order, b):
                for step in order:
                    kind = step[0]
                    if kind in ("LS", "LM", "LA"):
                        following = (b + 1) % NB
                        if kind == "LS":
                            ln.sums(dve, following, step[1])
                        elif kind == "LM":
                            ln.moments(dve, b, step[1])
                        else:
                            ln.apply(dve, b, following, step[1])
                    if kind == "TR":
                        m = step[1]
                        src = slots[slot_of[step] % 2][:, :, :].rearrange("p a n -> p (a n)")
                        tr_h.wait(dve, b, m + 1)
                        if m == 0:
                            dve.tensor_tensor(x0l[:, :], src[:, 0:N], x0h[:, :].bitcast(F32),
                                              ALU.subtract).then_inc(tr_l.sem, 1)
                        else:
                            dve.tensor_tensor(x1s[D1:P, :], src[D1:P, 0:N], x1s[D1:P, :].bitcast(F32),
                                              ALU.subtract).then_inc(tr_l.sem, 1)
                    elif kind == "V":
                        t = step[1]
                        v_h.wait(dve, b, t + 1)
                        for a in range(2):
                            src = v_halves(t)[a][0:TQ[t], 0:6 * HD].rearrange("p (h n) -> p h n", n=HD)
                            hs = slice(6 * a, 6 * a + 6)
                            last = dve.tensor_tensor(v_s[0:TQ[t], t, hs, HD:2 * HD], src,
                                                     v_s[0:TQ[t], t, hs, 0:HD].bitcast(F32), ALU.subtract)
                        last.then_inc(v_l.sem, 1)
                    elif kind == "QK":
                        p, m = step[1:]
                        proj_h.wait(dve, b, qk_index[step] + 1)
                        low = (k_l[:, p % 2, :] if m else q_l[:, :]).rearrange("p (a n) -> p a n", a=2)
                        dve.scalar_tensor_tensor(low, slot_view(slot_of[step], P, HALF), (1.0 if m else 0.125),
                                                 qk_h[:, m, :].rearrange("p (a n) -> p a n", a=2).bitcast(F32),
                                                 ALU.mult, ALU.subtract).then_inc(proj_l.sem, 1)
                    elif kind == "S":
                        n, i = step[1:]
                        tq = TQ[i]
                        full_wait(dve, b, step)
                        dve.tensor_reduce(negmax[0:tq, n, i:i + 1], slot_view(slot_of[step], tq, HALF), AXXY,
                                          ALU.max, negate=True).then_inc(max_ok.sem, 1)
                    elif kind == "T":
                        n, i = step[1:]
                        ptr_h.wait(dve, b, n * 6 + i + 1)
                        for (dst, src), (high, _) in zip(transposed(pt_l, bank_of[step], i),
                                                         transposed(pt_h, bank_of[step], i)):
                            last = dve.tensor_tensor(dst, src, high.bitcast(F32), ALU.subtract)
                        last.then_inc(ptr_l.sem, 1)
                        if i == 0:
                            exp_ok.wait(dve, b, (n + 1) * NTILE)
                            dve.reciprocal(rinv[:, n, :], rowsum[:, n, :]).then_inc(rinv_ok.sem, 1)
                    elif kind == "Y":
                        n = step[1]
                        rinv_ok.wait(dve, b, n + 1)
                        added.wait(dve, b, n)
                        full_wait(dve, b, step)
                        for t in range(2):
                            row = rows_of(h, b, t)
                            last = dve.scalar_tensor_tensor(row, slots[slot_of[step] % 2][:, 0, t * D:(t + 1) * D],
                                                            rinv[:, n, t:t + 1], row, ALU.mult, ALU.add)
                        last.then_inc(added.sem, 1)

            ln.whole(dve, -1, 0)
            run(PRO[:2], -1)
            dve.wait_ge(w_hi, 1)
            dve.tensor_tensor(w0l[:, :], stage[:, 0:W3], w0h[:, :].bitcast(F32), ALU.subtract).then_inc(w_lo, 1)
            dve.wait_ge(w_hi, 2)
            dve.tensor_tensor(w1l[:, :], stage[0:D1, W3:2 * W3], w1h[0:D1, :].bitcast(F32),
                              ALU.subtract).then_inc(w_lo, 1)
            run(PRO[2:], -1)
            with dve.Fori(0, NB) as b:
                run(dve_steps, b)

        @block.tensor
        def _(pe):
            for s in (slot_full, bank_full, o_full, v_full):
                s.start(pe)
            pe.wait_ge(ident_ok, 5)

            def run(order, b):
                for step in order:
                    kind = step[0]
                    done = slot_full.sem if not ahead(b) else pro_full
                    if step in slot_of:
                        slot = slots[slot_of[step] % 2]
                        if not ahead(b):
                            wait_slot_free(pe, b, slot_of[step])
                        elif PRO.index(step) == 1:
                            tr_l.wait(pe, b, 1)
                        elif PRO.index(step) == 3:
                            proj_l.wait(pe, b, qk_index[step])
                    if kind == "TR":
                        m = step[1]
                        ln.hn_ok.wait(pe, b, NTILE)
                        take_wait(pe, taken)
                        flat = slot[:, :, :].rearrange("p a n -> p (a n)")
                        for t, tq in enumerate(TQ):
                            last = pe.transpose(flat[:, t * P:t * P + tq], hn[0:tq, t, m * P:(m + 1) * P],
                                                ident[0:tq, 0:tq])
                        last.then_inc(done, 1)
                    elif kind == "V":
                        t = step[1]
                        if t == 0:
                            tr_l.wait(pe, b, 0)
                            o_out.wait(pe, b, 0)
                        elif t == 1:
                            ptr_l.wait(pe, b, 0)
                            scaled_ok.wait(pe, b, 0)
                        else:
                            v_l.wait(pe, b, t - 1)
                        rows = slice(t * P, t * P + TQ[t])
                        for a in range(2):
                            cols = slice(2 * NH * HD + a * 6 * HD, 2 * NH * HD + (a + 1) * 6 * HD)
                            terms = [(x0h[:, rows], w0h[:, cols]), (x0l[:, rows], w0h[:, cols]),
                                     (x0h[:, rows], w0l[:, cols]), (x1s[:, rows], w1h[:, cols]),
                                     (x1s[0:D1, rows], w1l[:, cols])]
                            for j, (lhs, rhs) in enumerate(terms):
                                last = pe.matmul(v_halves(t)[a][0:TQ[t], 0:6 * HD], lhs, rhs,
                                                 start=(j == 0), stop=(j == 4))
                        last.then_inc(v_full.sem, 1)
                    elif kind == "QK":
                        p, m = step[1:]
                        if p == 0:
                            tr_l.wait(pe, b, 2)
                        cols = slice(m * NH * HD + p * P, m * NH * HD + (p + 1) * P)
                        for a in range(2):
                            rows = slice(a * HALF, (a + 1) * HALF)
                            terms = [(w0h[:, cols], x0h[:, rows]), (w0h[:, cols], x0l[:, rows]),
                                     (w0l[:, cols], x0h[:, rows]), (w1h[:, cols], x1s[:, rows]),
                                     (w1l[:, cols], x1s[0:D1, rows])]
                            for j, (lhs, rhs) in enumerate(terms):
                                last = pe.matmul(slot[:, a, 0:HALF], lhs, rhs, start=(j == 0), stop=(j == 4))
                        last.then_inc(done, 1)
                    elif kind == "S":
                        n, i = step[1:]
                        tq, par, e = TQ[i], n // 2 % 2, n % 2
                        if i == 0 and e == 0:
                            stacked[par].wait(pe, b, stack_count(n // 2))
                            proj_l.wait(pe, b, n)
                        q = slice(i * P, i * P + tq)
                        own = slice(e * HD, (e + 1) * HD)
                        for a in range(2):
                            k = slice(a * HALF, (a + 1) * HALF)
                            pe.matmul(slot[0:tq, a, 0:HALF], q_s[:, par, e, q], k_s[:, par, e, k], start=True, stop=False)
                            last = pe.matmul(slot[0:tq, a, 0:HALF], q_s[own, par, e, q], k_l[own, par, k],
                                             start=False, stop=True)
                        last.then_inc(done, 1)
                    elif kind == "T":
                        n, i = step[1:]
                        k = bank_of[step]
                        wait_bank_free(pe, b, k)
                        if k == 0:
                            v_l.wait(pe, b, NTILE)
                        exp_ok.wait(pe, b, (n + 1) * NTILE)
                        take_wait(pe, taken)
                        bank = banks[k % 2]
                        if i == 0:
                            for t, kw in enumerate(TQ):
                                last = pe.transpose(bank[0:kw, t * NT:(t + 1) * NT],
                                                    prob[0:NT, n % 2, 4, t * P:t * P + kw], ident[0:NT, 0:NT])
                        else:
                            kw = TQ[i - 1]
                            for t in range(4):
                                last = pe.transpose(bank[0:kw, t * P:(t + 1) * P],
                                                    prob[:, n % 2, t, (i - 1) * P:(i - 1) * P + kw], ident[:, :])
                        last.then_inc(bank_full.sem, 1)
                    elif kind == "PV":
                        n, t = step[1:]
                        ptr_l.wait(pe, b, n * 6 + t + 2)
                        if t == 0:
                            v_l.wait(pe, b, NTILE)
                            o_out.wait(pe, b, n)
                        kw = TQ[t]
                        for a in range(2):
                            q = slice(a * HALF, (a + 1) * HALF)
                            pe.matmul(o_ps[:, a, 0:HALF], v_s[0:kw, t, n, :], pt_h[0:kw, t, q],
                                      start=(t == 0), stop=False)
                            last = pe.matmul(o_ps[:, a, 0:HALF], v_s[0:kw, t, n, :], pt_l[0:kw, t, q],
                                             start=False, stop=(t == NTILE - 1))
                        if t == NTILE - 1:
                            last.then_inc(o_full.sem, 1)
                    elif kind == "Y":
                        n = step[1]
                        o_out.wait(pe, b, n + 1)
                        for t, tq in enumerate(TQ):
                            if t < 4:
                                dst = slot[0:tq, t // 2, (t % 2) * D:(t % 2 + 1) * D]
                            else:
                                wait_bank_free(pe, b, bank_of[step])
                                dst = banks[bank_of[step] % 2][0:tq, 0:D]
                            rows = slice(t * P, t * P + tq)
                            last = pe.matmul(dst, o_s[:, rows], wo[:, n, :], start=True, stop=True)
                            if t == 3:
                                last.then_inc(done, 1)
                        last.then_inc(bank_full.sem, 1)

            run(PRO[:2], -1)
            pe.wait_ge(w_lo, 2)
            run(PRO[2:], -1)
            pe.wait_ge(w_in[2], 16)
            with pe.Fori(0, NB) as b:
                run(steps, b)


def ffn_order():
    order = [("L", t, 0) for t in range(NTILE)]
    order += [("L", 0, 1), ("LT", 0), ("LT", 1), ("LT", 2), ("L", 1, 1), ("LT", 3), ("L", 2, 1), ("L", 3, 1), ("L", 4, 1)]
    order += [("DT", t, 0) for t in range(NTILE)]
    order += [("LT", 4), ("LT", 5), ("LT", 6), ("LT", 7), ("SL", 0, 0), ("SL", 1, 0)]
    order += [("DT", t, 1) for t in range(NTILE)]
    order += [("CT", 0), ("CT", 1), ("CT", 2), ("SL", 0, 1), ("CT", 3), ("CT", 4), ("SL", 1, 1)]
    order += [("CT", 5), ("CT", 6), ("CT", 7)]
    for e in range(NE):
        order += [("H", e, 0), ("H", e, 1)] + ([("Y", e - 1)] if e else [])
    return order + [("TR", 0), ("TR", 1), ("Y", NE - 1)] + [("O", t) for t in range(NTILE)]


def ffn_phase(nc, sem, h, aps):
    phi0_d, phi1_d, w1a_d, w1b_d, b1_d, w2_d, b2_d, out_d = aps
    order = ffn_order()
    NU = len(order)
    at = {u: i for i, u in enumerate(order)}
    nth = {u: [v for v in order if v[0] == u[0]].index(u) + 1 for u in order}
    HS = ES // 2
    with ExitStack() as ctx:
        def sb(name, shape, dt=F32):
            return ctx.enter_context(nc.sbuf_tensor(name, shape, dt))

        def shared(name, shape, other, other_shape):
            with nc.sbuf_tensor(other, other_shape, F32R) as turns:
                pass
            return sb(name, shape), turns
        ident = sb("ff_ident", [P, P])
        hn, hn_l = shared("ff_hn", [P, NTILE, 2 * P], "ff_hn_l", [P, NTILE, 2 * P])
        stats = sb("ff_stats", [P, NTILE, 6])
        mv = sb("ff_mv", [P, NTILE, 2])
        rstd = sb("ff_rstd", [P, 3, NTILE])
        phi0h, phi0l, phi1s = (sb(n, [P, ES], F32R) for n in ("ff_phi0h", "ff_phi0l", "ff_phi1s"))
        w0h, w0l, w1s = (sb(n, [P, NE, FH], F32R) for n in ("ff_w0h", "ff_w0l", "ff_w1s"))
        rows_or_low = sb("ff_rows_or_low", [P, NTILE * (ES // 2)], F32R)
        x0h, x0l, x1h = (rows_or_low[:, i * N:(i + 1) * N] for i in range(3))
        x1l = rows_or_low[0:D1, 3 * N:4 * N]
        dt_low = rows_or_low[:, :].rearrange("p (t n) -> p t n", t=NTILE)
        s0h, s0l, s1h = (sb(n, [P, ES], F32R) for n in ("ff_s0h", "ff_s0l", "ff_s1h"))
        s1l = sb("ff_s1l", [D1, ES], F32R)
        b1, b2 = sb("ff_b1", [P, NE * FM]), sb("ff_b2", [P, NE, D])
        w2 = sb("ff_w2", [P, NE, FM, D])
        logit, dt1 = shared("ff_logit", [P, NTILE, ES], "ff_dt1", [P, NTILE, ES])
        comb = sb("ff_comb", [P, NTILE, ES])
        disp = sb("ff_disp", [P, NM, N])
        hid, dt0 = shared("ff_hid", [P, 2, FM, NS], "ff_dt0", [P, NTILE, ES // 2])
        y, hn_h = shared("ff_y", [P, NM, D], "ff_hn_h", [P, NTILE, 2 * P])
        nmc, sumc, rc = (sb(n, [P, NTILE]) for n in ("ff_nmc", "ff_sumc", "ff_rc"))
        nmh = sb("ff_nmh", [P, NTILE, 2])
        nmd, sumd, rd = (sb(n, [P, NM]) for n in ("ff_nmd", "ff_sumd", "ff_rd"))
        slots = [ctx.enter_context(nc.psum_tensor(f"ff_slot{i}", [P, 1024], F32)) for i in range(4)]
        stage_a = logit[:, :, :].rearrange("p t n -> p (t n)")
        stage_b = comb[:, :, :].rearrange("p t n -> p (t n)")
        stage_phi0, stage_phi1 = stage_a[:, 0:ES], stage_a[:, ES:2 * ES]
        stage_w0, stage_w1 = stage_a[:, 2 * ES:2 * ES + NE * FH], stage_b[:, 0:NE * FH]

        phi_in, w1_in, w2_in, b_in = (sem(n) for n in ("ff_phi_in", "ff_w1_in", "ff_w2_in", "ff_b_in"))
        w_hi, w_lo = sem("ff_w_hi"), sem("ff_w_lo")
        const_ok = sem("ff_const")
        taken = sem("ff_taken")
        pro_full = sem("ff_pro_full")
        ln = LayerNorm(sem, "ff_ln", h, hn, stats, mv, rstd)
        full = Tally(sem("ff_full"), NU)
        tr_h, tr_l = Tally(sem("ff_tr_h"), 2), Tally(sem("ff_tr_l"), 2)
        maxc = Tally(sem("ff_maxc"), 1)
        half_max = Tally(sem("ff_half_max"), 2 * NTILE)
        logit_out = Tally(sem("ff_logit_out"), 2 * NTILE)
        comb_ok = Tally(sem("ff_comb_ok"), NTILE)
        rc_ok = Tally(sem("ff_rc_ok"), 1)
        maxd = Tally(sem("ff_maxd"), NM)
        disp_exp = Tally(sem("ff_disp_exp"), NM)
        rd_ok = Tally(sem("ff_rd_ok"), NM)
        pool_tiles = (0, 4, 5)
        dve_tiles = [m for m in range(NM) if m not in pool_tiles]
        dve_scaled = Tally(sem("ff_dve_scaled"), len(dve_tiles))
        pool_scaled = Tally(sem("ff_pool_scaled"), len(pool_tiles))
        ct_out = Tally(sem("ff_ct_out"), NM)
        dt_out, dt_low_out = Tally(sem("ff_dt_out"), 2 * NTILE), Tally(sem("ff_dt_low_out"), 2 * NTILE)
        hn_high, hn_low = Tally(sem("ff_hn_high"), NTILE), Tally(sem("ff_hn_low"), NTILE)
        sl_h, sl_l = Tally(sem("ff_sl_h"), 4), Tally(sem("ff_sl_l"), 4)
        hid_ok = Tally(sem("ff_hid_ok"), 2 * NE)
        y_ok = Tally(sem("ff_y_ok"), NE)
        fin_ok = Tally(sem("ff_fin_ok"), NTILE)
        sent = Tally(sem("ff_sent"), 32)
        block = ctx.enter_context(nc.Block())

        def inverse(dve, b, m):
            disp_exp.wait(dve, b, m + 1)
            dve.reciprocal(rd[:, m:m + 1], sumd[:, m:m + 1]).then_inc(rd_ok.sem, 1)

        def normalise(eng, b, m):
            rd_ok.wait(eng, b, m + 1)
            take_wait(eng, ln.taken if m in pool_tiles else taken)
            eng.tensor_scalar(disp[:, m, :], disp[:, m, :], rd[:, m:m + 1], None,
                              ALU.mult).then_inc((pool_scaled if m in pool_tiles else dve_scaled).sem, 1)

        def released(u):
            reader = {"TR": tr_l, "L": logit_out, "LT": disp_exp, "CT": ct_out, "DT": dt_low_out, "SL": sl_l,
                      "H": hid_ok, "Y": y_ok, "O": fin_ok}[u[0]]
            return reader, nth[u]

        def slot(u):
            return slots[at[u] % 4]

        def dispatch(t, a):
            return dt0[0:TQ[t], t, :] if a == 0 else dt1[0:TQ[t], t, HS:ES]

        def full_wait(eng, it, u):
            if ahead(it):
                eng.wait_ge(pro_full, u[1] + 1)
            else:
                full.wait(eng, it, at[u] + 1)

        def slot_free(pe, b, u):
            if ahead(b):
                return
            k, back = at[u], 1
            while (k - back) % NU % 4 != k % 4:
                back += 1
            unit = order[(k - back) % NU]
            if (u[0], unit[0]) in (("H", "SL"), ("Y", "H")) or unit == ("Y", NE - 1):
                return
            tally, count = released(unit)
            tally.wait(pe, b, count - (tally.per if k < back else 0))
            take_wait(pe, taken)

        def parts_of(e, m):
            ms, ss = slice(m * P, (m + 1) * P), slice(e * NS, (e + 1) * NS)
            return ((w0h[:, e, ms], s0h[:, ss]), (w0l[:, e, ms], s0h[:, ss]), (w0h[:, e, ms], s0l[:, ss]),
                    (w1s[:, e, ms], s1h[:, ss]), (w1s[0:D1, e, ms], s1l[:, ss]))

        @block.sync
        def _(sp):
            sp.dma_start(stage_phi0, phi0_d).then_inc(phi_in, 16)
            sp.dma_start(stage_phi1, phi1_d).then_inc(phi_in, 16)
            sp.dma_start(stage_w0, w1a_d).then_inc(w1_in, 16)
            sp.dma_start(stage_w1, w1b_d).then_inc(w1_in, 16)
            sp.dma_start(b1[:, :], b1_d).then_inc(b_in, 16)
            sp.dma_start(b2[:, :, :].rearrange("p e d -> p (e d)"), b2_d).then_inc(b_in, 16)
            sp.dma_start(w2[:, :, :, :].rearrange("p e m d -> p (e m d)"), w2_d).then_inc(w2_in, 16)
            sent.start(sp)
            with sp.Fori(0, NB) as b:
                main = out_d[bass.ds(b, 1), 0:NX, :].rearrange("o (t p) d -> p (o t) d", p=P)
                tail = out_d[bass.ds(b, 1), NX:N, :].rearrange("o n d -> (o n) d")
                rows = h[:, bass.ds(b * NTILE, NTILE - 1), :]
                last = rows_of(h, b, NTILE - 1)
                fin_ok.wait(sp, b, NTILE)
                take_wait(sp, taken)
                sp.dma_start(main, rows).then_inc(sent.sem, 16)
                sp.dma_start(tail, last).then_inc(sent.sem, 16)
            sp.wait_ge(sent.sem, (NB + 1) * 32)

        @block.gpsimd
        def _(pool):
            ln.rstd_ok.start(pool, 2)
            pool.memset(ident[:, :], 0.0).then_inc(const_ok, 1)
            pool.memset(rstd[:, :, :], -0.5).then_inc(const_ok, 1)
            pool.memset(mv[:, :, :], 1.0).then_inc(const_ok, 1)
            pool.memset(sumc[:, :], 1.0).then_inc(const_ok, 1)
            pool.memset(nmh[:, :, :], 0.0).then_inc(const_ok, 1)
            pool.wait_ge(const_ok, 5)
            pool.affine_select(out=ident[:, :], in_=ident[:, :], compare_op=ALU.not_equal, fill=1.0, base=0,
                               pattern=[[-1, P]], channel_multiplier=1).then_inc(const_ok, 1)
            ln.scale(pool, -1)
            pool_scaled.start(pool)
            with pool.Fori(0, NB) as b:
                for m in pool_tiles:
                    normalise(pool, b, m)
                ln.scale(pool, b)

        @block.scalar
        def _(act):
            for s in (hn_high, logit_out, comb_ok, disp_exp, dt_out, sl_h, hid_ok):
                s.start(act)
            tr_h.start(act, 2)
            def high(b, u):
                full_wait(act, b, u)
                act.activation((x1h if u[1] else x0h)[:, :], slot(u)[:, 0:N], ACT.Copy).then_inc(tr_h.sem, 1)

            high(-1, ("TR", 0))
            high(-1, ("TR", 1))
            act.wait_ge(phi_in, 32)
            act.activation(phi0h[:, :], stage_phi0, ACT.Copy).then_inc(w_hi, 1)
            act.activation(phi1s[:, :], stage_phi1, ACT.Copy).then_inc(w_hi, 1)
            act.wait_ge(w1_in, 32)
            act.activation(w0h[:, :, :].rearrange("p e m -> p (e m)"), stage_w0, ACT.Copy).then_inc(w_hi, 1)
            act.activation(w1s[:, :, :].rearrange("p e m -> p (e m)"), stage_w1, ACT.Copy).then_inc(w_hi, 1)
            act.wait_ge(w_lo, 4)
            act.wait_ge(b_in, 32)
            with act.Fori(0, NB) as b:
                for u in order:
                    kind = u[0]
                    if kind == "TR":
                        high(b, u)
                    elif kind == "L":
                        t, tq = u[1], TQ[u[1]]
                        cs = slice(u[2] * HS, (u[2] + 1) * HS)
                        if u[2] == 0:
                            full.wait(act, b, at[u] + 1)
                            act.activation(hn_h[0:tq, t, :], hn[0:tq, t, :], ACT.Copy).then_inc(hn_high.sem, 1)
                        half_max.wait(act, b, nth[u])
                        act.activation(logit[0:tq, t, cs], slot(u)[0:tq, 0:HS], ACT.Copy).then_inc(logit_out.sem, 1)
                    elif kind == "LT":
                        m = u[1]
                        maxd.wait(act, b, m + 1)
                        act.activation(disp[:, m, :], slot(u)[:, 0:N], ACT.Exp, bias=nmd[:, m:m + 1],
                                       accum_out=sumd[:, m:m + 1]).then_inc(disp_exp.sem, 1)
                    elif kind == "DT":
                        t, a = u[1:]
                        if a == 1:
                            comb_ok.wait(act, b, t + 1)
                            take_wait(act, taken)
                        full.wait(act, b, at[u] + 1)
                        act.activation(dispatch(t, a), slot(u)[0:TQ[t], 0:HS],
                                       ACT.Copy).then_inc(dt_out.sem, 1)
                    elif kind == "SL" and u[2] == 1:
                        cs = slice(u[2] * HS, (u[2] + 1) * HS)
                        full.wait(act, b, at[u] + 1)
                        act.activation((s1h if u[1] else s0h)[:, cs], slot(u)[:, 0:HS], ACT.Copy).then_inc(sl_h.sem, 1)
                    elif kind == "H":
                        e, part = u[1:]
                        full.wait(act, b, at[u] + 1)
                        ms = range(4) if part == 0 else range(4, FM)
                        for m in ms:
                            last = act.activation(hid[:, e % 2, m, :], slot(u)[:, (m - ms[0]) * NS:(m - ms[0] + 1) * NS],
                                                  ACT.Gelu_apprx_tanh, bias=b1[:, e * FM + m:e * FM + m + 1])
                        last.then_inc(hid_ok.sem, 1)
                    for i in (range(NTILE) if u == ("LT", NM - 1) else ()):
                        tq = TQ[i]
                        maxc.wait(act, b, 1)
                        act.activation(comb[0:tq, i, :], logit[0:tq, i, :], ACT.Exp, bias=nmc[0:tq, i:i + 1],
                                       accum_out=sumc[0:tq, i:i + 1]).then_inc(comb_ok.sem, 1)

        @block.vector
        def _(dve):
            ln.start(dve, True)
            for s in (half_max, maxc, rc_ok, maxd, rd_ok, dve_scaled, hn_low, dt_low_out, ct_out, sl_l, y_ok, fin_ok):
                s.start(dve)
            tr_l.start(dve, 2)
            dve.wait_ge(const_ok, 6)
            ln.whole(dve, -1, 0)
            def low(b, u):
                dst, hi = ((x0l, x0h), (x1l, x1h))[u[1]]
                rows = dst.shape[0]
                tr_h.wait(dve, b, u[1] + 1)
                dve.tensor_tensor(dst[:, :], slot(u)[0:rows, 0:N], hi[0:rows, :].bitcast(F32),
                                  ALU.subtract).then_inc(tr_l.sem, 1)

            low(-1, ("TR", 0))
            low(-1, ("TR", 1))
            dve.wait_ge(w_hi, 2)
            dve.tensor_tensor(phi0l[:, :], stage_phi0, phi0h[:, :].bitcast(F32), ALU.subtract).then_inc(w_lo, 1)
            dve.tensor_tensor(phi1s[D1:P, :], stage_phi1[D1:P], phi1s[D1:P, :].bitcast(F32),
                              ALU.subtract).then_inc(w_lo, 1)
            dve.wait_ge(w_hi, 4)
            dve.tensor_tensor(w0l[:, :, :].rearrange("p e m -> p (e m)"), stage_w0,
                              w0h[:, :, :].rearrange("p e m -> p (e m)").bitcast(F32), ALU.subtract).then_inc(w_lo, 1)
            dve.tensor_tensor(w1s[D1:P, :, :].rearrange("p e m -> p (e m)"), stage_w1[D1:P],
                              w1s[D1:P, :, :].rearrange("p e m -> p (e m)").bitcast(F32),
                              ALU.subtract).then_inc(w_lo, 1)
            dve.wait_ge(b_in, 32)
            with dve.Fori(0, NB) as b:
                following = (b + 1) % NB
                for u in order:
                    kind = u[0]
                    if kind == "TR":
                        low(b, u)
                    elif kind == "L":
                        t, tq = u[1], TQ[u[1]]
                        full.wait(dve, b, at[u] + 1)
                        dve.tensor_reduce(nmh[0:tq, t, u[2]:u[2] + 1], slot(u)[0:tq, 0:HS], AXX, ALU.max,
                                          negate=True).then_inc(half_max.sem, 1)
                        if u[2] == 0:
                            hn_high.wait(dve, b, t + 1)
                            dve.tensor_tensor(hn_l[0:tq, t, :], hn[0:tq, t, :],
                                              hn_h[0:tq, t, :].bitcast(F32), ALU.subtract).then_inc(hn_low.sem, 1)
                        if u == ("L", NTILE - 1, 1):
                            half_max.wait(dve, b, nth[u])
                            dve.tensor_tensor(nmc[:, :], nmh[:, :, 0], nmh[:, :, 1], ALU.min).then_inc(maxc.sem, 1)
                    elif kind == "DT":
                        t, a = u[1:]
                        tq = TQ[t]
                        dt_out.wait(dve, b, nth[u])
                        dve.tensor_tensor(dt_low[0:tq, t, :], slot(u)[0:tq, 0:HS], dispatch(t, a).bitcast(F32),
                                          ALU.subtract).then_inc(dt_low_out.sem, 1)
                    elif kind == "LT":
                        m = u[1]
                        full.wait(dve, b, at[u] + 1)
                        dve.tensor_reduce(nmd[:, m:m + 1], slot(u)[:, 0:N], AXX, ALU.max,
                                          negate=True).then_inc(maxd.sem, 1)
                    elif kind == "CT":
                        m = u[1]
                        full.wait(dve, b, at[u] + 1)
                        dve.tensor_copy(disp[:, m, :], slot(u)[:, 0:N]).then_inc(ct_out.sem, 1)
                    elif kind == "SL":
                        cs = slice(u[2] * HS, (u[2] + 1) * HS)
                        dst, hi = ((s0l, s0h), (s1l, s1h))[u[1]]
                        rows = dst.shape[0]
                        if u[2] == 0:
                            full.wait(dve, b, at[u] + 1)
                            dve.tensor_copy(hi[:, cs], slot(u)[:, 0:HS]).then_inc(sl_h.sem, 1)
                        sl_h.wait(dve, b, nth[u])
                        dve.tensor_tensor(dst[:, cs], slot(u)[0:rows, 0:HS], hi[0:rows, cs].bitcast(F32),
                                          ALU.subtract).then_inc(sl_l.sem, 1)
                    done = {("L", 1, 1): (0, 1), ("L", 2, 1): (2, 3), ("LT", 5): (4,), ("LT", 6): (5,),
                            ("LT", 7): (6, 7)}
                    for m in done.get(u, ()):
                        inverse(dve, b, m)
                        if m in dve_tiles:
                            normalise(dve, b, m)
                    if kind == "Y":
                        e = u[1]
                        full.wait(dve, b, at[u] + 1)
                        for st in range(2):
                            last = dve.tensor_tensor(y[:, 2 * e + st, :], slot(u)[:, st * D:(st + 1) * D],
                                                     b2[:, e, :], ALU.add)
                        last.then_inc(y_ok.sem, 1)
                    elif kind == "O":
                        t, tq = u[1], TQ[u[1]]
                        if t == 0:
                            comb_ok.wait(dve, b, NTILE)
                            dve.reciprocal(rc[:, :], sumc[:, :]).then_inc(rc_ok.sem, 1)
                            rc_ok.wait(dve, b, 1)
                        full.wait(dve, b, at[u] + 1)
                        row = rows_of(h, b, t)
                        dve.scalar_tensor_tensor(row, slot(u)[0:tq, 0:D], rc[0:tq, t:t + 1], row,
                                                 ALU.mult, ALU.add).then_inc(fin_ok.sem, 1)
                    elif kind == "H" and u[2] == 1 and u[1] < 3:
                        for t in range(NTILE):
                            if u[1] == 0:
                                ln.sums(dve, following, t)
                            elif u[1] == 1:
                                ln.moments(dve, b, t)
                            else:
                                ln.apply(dve, b, following, t)

        @block.tensor
        def _(pe):
            full.start(pe)
            pe.wait_ge(const_ok, 6)

            def product(out, parts):
                for i, (a, z) in enumerate(parts):
                    last = pe.matmul(out, a, z, start=(i == 0), stop=(i == len(parts) - 1))
                return last

            def transposes(b, u):
                m, out = u[1], slot(u)
                ln.hn_ok.wait(pe, b, NTILE)
                take_wait(pe, taken)
                for t, tq in enumerate(TQ):
                    last = pe.transpose(out[:, t * P:t * P + tq], hn[0:tq, t, m * P:(m + 1) * P], ident[0:tq, 0:tq])
                return last

            for m in range(2):
                transposes(-1, ("TR", m)).then_inc(pro_full, 1)
            pe.wait_ge(w_lo, 2)
            with pe.Fori(0, NB) as b:
                for u in order:
                    kind = u[0]
                    out = slot(u)
                    slot_free(pe, b, u)
                    if kind == "TR":
                        last = transposes(b, u)
                    elif kind == "L":
                        t, tq = u[1], TQ[u[1]]
                        ts, cs = slice(t * P, t * P + tq), slice(u[2] * HS, (u[2] + 1) * HS)
                        if t == 0 and u[2] == 0:
                            tr_l.wait(pe, b, 0)
                        last = product(out[0:tq, 0:HS], (
                            (x0h[:, ts], phi0h[:, cs]), (x0h[:, ts], phi0l[:, cs]), (x0l[:, ts], phi0h[:, cs]),
                            (x1h[:, ts], phi1s[:, cs]), (x1l[:, ts], phi1s[0:D1, cs])))
                    elif kind == "LT":
                        logit_out.wait(pe, b, nth[("L", NTILE - 1, u[1] // (NM // 2))])
                        take_wait(pe, taken)
                        for t, tq in enumerate(TQ):
                            last = pe.transpose(out[:, t * P:t * P + tq], logit[0:tq, t, u[1] * P:(u[1] + 1) * P],
                                                ident[0:tq, 0:tq])
                    elif kind == "CT":
                        comb_ok.wait(pe, b, NTILE)
                        take_wait(pe, taken)
                        for t, tq in enumerate(TQ):
                            last = pe.transpose(out[:, t * P:t * P + tq], comb[0:tq, t, u[1] * P:(u[1] + 1) * P],
                                                ident[0:tq, 0:tq])
                    elif kind == "DT":
                        t, a = u[1:]
                        dve_scaled.wait(pe, b, len([m for m in dve_tiles if m < (a + 1) * NM // 2]))
                        pool_scaled.wait(pe, b, len([m for m in pool_tiles if m < (a + 1) * NM // 2]))
                        take_wait(pe, taken)
                        for m in range(NM // 2):
                            last = pe.transpose(out[0:TQ[t], m * P:(m + 1) * P],
                                                disp[:, a * NM // 2 + m, t * P:t * P + TQ[t]], ident[:, :])
                    elif kind == "SL":
                        ds = slice(u[1] * P, (u[1] + 1) * P)
                        hn_low.wait(pe, b, NTILE)
                        dt_low_out.wait(pe, b, nth[("DT", NTILE - 1, u[2])])
                        parts = []
                        for t, tq in enumerate(TQ):
                            high = dispatch(t, u[2])
                            parts += [(hn_h[0:tq, t, ds], high), (hn_l[0:tq, t, ds], high),
                                      (hn_h[0:tq, t, ds], dt_low[0:tq, t, :])]
                        last = product(out[:, 0:HS], parts)
                    elif kind == "H":
                        e, part = u[1:]
                        if u == ("H", 0, 0):
                            pe.wait_ge(w_lo, 4)
                            pe.wait_ge(w2_in, 16)
                        sl_l.wait(pe, b, 4)
                        ms = range(4) if part == 0 else range(4, FM)
                        for m in ms:
                            last = product(out[:, (m - ms[0]) * NS:(m - ms[0] + 1) * NS], parts_of(e, m))
                    elif kind == "Y":
                        e = u[1]
                        hid_ok.wait(pe, b, 2 * e + 2)
                        for st in range(2):
                            for m in range(FM):
                                last = pe.matmul(out[:, st * D:(st + 1) * D], hid[:, e % 2, m, st * P:(st + 1) * P],
                                                 w2[:, e, m, :], start=(m == 0), stop=(m == FM - 1))
                    elif kind == "O":
                        t, tq = u[1], TQ[u[1]]
                        ct_out.wait(pe, b, NM)
                        if t > 0:
                            y_ok.wait(pe, b, NE)
                        for m in range(NM):
                            if t == 0 and m == NM - 2:
                                y_ok.wait(pe, b, NE)
                            last = pe.matmul(out[0:tq, 0:D], disp[:, m, t * P:t * P + tq], y[:, m, :],
                                             start=(m == 0), stop=(m == NM - 1))
                    last.then_inc(full.sem, 1)


def early_fusion_kernel(nc, x_d, txt_d, f_d, wtok_d, w0_d, w1_d, wo_d,
                        phi0_d, phi1_d, w1a_d, w1b_d, b1_d, w2_d, b2_d, out_d):
    with ExitStack() as ctx:
        def sem(name):
            return ctx.enter_context(nc.semaphore(name))
        h = ctx.enter_context(nc.sbuf_tensor("h", [P, NB * NTILE, D], F32))
        tok_phase(nc, sem, h, (x_d, wtok_d, f_d, txt_d))
        attn_phase(nc, sem, h, (w0_d, w1_d, wo_d))
        ffn_phase(nc, sem, h, (phi0_d, phi1_d, w1a_d, w1b_d, b1_d, w2_d, b2_d, out_d))


def laid_out(x, txt, freq, w_tok, w_qkv, w_o, phi, w1, b1, w2, b2):
    import numpy as np
    c = np.ascontiguousarray
    xt = x.reshape(NB, NX, 3 * D).transpose(0, 2, 1)
    full = (CH - 1) * P
    x_l = np.concatenate([xt[:, :full].reshape(NB, CH - 1, P, NX),
                          np.concatenate([xt[:, full:], xt[:, full:]], 1)[:, None]], 1)
    wt = w_tok.reshape(D, 3 * D, 2, BANDS).transpose(2, 3, 1, 0)
    units = [wt[kind, 2 * jp + jj, ch * P:(ch + 1) * P]
             for ch in range(CH - 1) for jp in range(3) for kind in range(2) for jj in range(2)]
    units += [np.concatenate([wt[0, j, full:], wt[1, j, full:]]) for j in range(BANDS)]
    qkv = w_qkv.transpose(2, 1, 0, 3).reshape(D, 3 * NH * HD)
    wo = w_o.reshape(NH, HD, D).transpose(1, 0, 2).reshape(HD, NH * D)
    phi_t = phi.reshape(ES, D).T
    w1_t = w1.transpose(1, 0, 2).reshape(D, NE * FH)
    return {
        "x": c(x_l), "txt": c(txt), "freq": c(np.broadcast_to(freq, (P, BANDS))),
        "w_tok": c(np.stack(units, 1).reshape(P, NKU * D)),
        "w_qkv0": c(qkv[:P]), "w_qkv1": c(np.concatenate([qkv[P:], qkv[P:]])), "w_o": c(np.concatenate([wo, wo])),
        "phi0": c(phi_t[:P]), "phi1": c(np.concatenate([phi_t[P:], phi_t[P:]])),
        "w1a": c(w1_t[:P]), "w1b": c(np.concatenate([w1_t[P:], w1_t[P:]])),
        "b1": c(b1.reshape(NE * FM, P).T),
        "w2": c(w2.reshape(NE, FM, P, D).transpose(2, 0, 1, 3).reshape(P, NE * FM * D)),
        "b2": c(np.broadcast_to(b2.reshape(1, NE * D), (P, NE * D))),
    }


def kernel(x, txt, L0_tok_freq_bands, L0_tok_W, L0_attn_w_qkv, L0_attn_w_o, L0_ffn_phi, L0_ffn_w1,
           L0_ffn_b1, L0_ffn_w2, L0_ffn_b2):
    import numpy as np
    import concourse.bacc as bacc
    from concourse.bass_utils import run_bass_kernel_spmd

    given = [np.asarray(a) for a in (x, txt, L0_tok_freq_bands, L0_tok_W, L0_attn_w_qkv, L0_attn_w_o, L0_ffn_phi,
                                     L0_ffn_w1, L0_ffn_b1, L0_ffn_w2, L0_ffn_b2)]
    nc = bacc.Bacc("TRN2", target_bir_lowering=False, num_devices=1)
    arrays, args = {}, []
    for name, a in laid_out(*given).items():
        arrays[f"in_{name}_dram"] = a
        args.append(nc.dram_tensor(f"in_{name}_dram", a.shape, mybir.dt.from_np(a.dtype), kind="ExternalInput").ap())
    args.append(nc.dram_tensor("out_0_dram", (NB, N, D), F32, kind="ExternalOutput").ap())
    early_fusion_kernel(nc, *args)
    r = run_bass_kernel_spmd(nc, [arrays], core_ids=[0])
    return r.results[0]["out_0_dram"]
```
